# Optimizing a Trainium2 kernel written in Bass

```python
import numpy as np
import jax
import jax.numpy as jnp

def _softmax(x, axis=-1):
    return jax.nn.softmax(x, axis=axis)

def _gelu(x):
    return jax.nn.gelu(x, approximate=True)

def _silu(x):
    return jax.nn.silu(x)

def _sigmoid(x):
    return jax.nn.sigmoid(x)

def _layernorm(x, axis=-1, eps=1e-05):
    m = jnp.mean(x, axis=axis, keepdims=True)
    v = jnp.var(x, axis=axis, keepdims=True)
    return (x - m) / jnp.sqrt(v + eps)

def _scatter_add(tgt, idx, src, axis=0):
    return tgt.at[idx].add(src)

def _segment_sum(src, seg, n):
    return jax.ops.segment_sum(src, seg, n)
kernel_name = 'mk_dlrm_tower_d1_rec_r8_43e828'

def setup_inputs(seed: int=0):
    np.random.seed(seed)
    _w = jnp.asarray

    def _rec_inputs():
        import jax
        import jax.numpy as jnp
        _tk = jax.random.key(seed)
        dense_ctx = jax.random.normal(jax.random.fold_in(_tk, 190), (512, 16), jnp.float32)
        ids = jnp.stack([jax.random.randint(jax.random.fold_in(_tk, 200 + f), (512,), 0, v, jnp.int32) for f, v in enumerate([125000, 1000, 1250, 12500, 1250, 12500, 125000, 1250, 1250, 12500, 125000, 125000, 12500, 1000, 12500, 125000, 12500, 12500, 12500, 1250, 12500, 12500, 1250, 125000, 1000, 12500, 12500, 1000, 1000, 12500, 12500, 1000, 1000, 1000, 12500, 1250, 12500, 12500, 1250])], axis=1)
        tbl_0 = 0.05 * jax.random.normal(jax.random.fold_in(_tk, 500 + 0), (125000, 32), jnp.float32)
        tbl_1 = 0.05 * jax.random.normal(jax.random.fold_in(_tk, 500 + 1), (1000, 32), jnp.float32)
        tbl_2 = 0.05 * jax.random.normal(jax.random.fold_in(_tk, 500 + 2), (1250, 32), jnp.float32)
        tbl_3 = 0.05 * jax.random.normal(jax.random.fold_in(_tk, 500 + 3), (12500, 32), jnp.float32)
        tbl_4 = 0.05 * jax.random.normal(jax.random.fold_in(_tk, 500 + 4), (1250, 32), jnp.float32)
        tbl_5 = 0.05 * jax.random.normal(jax.random.fold_in(_tk, 500 + 5), (12500, 32), jnp.float32)
        tbl_6 = 0.05 * jax.random.normal(jax.random.fold_in(_tk, 500 + 6), (125000, 32), jnp.float32)
        tbl_7 = 0.05 * jax.random.normal(jax.random.fold_in(_tk, 500 + 7), (1250, 32), jnp.float32)
        tbl_8 = 0.05 * jax.random.normal(jax.random.fold_in(_tk, 500 + 8), (1250, 32), jnp.float32)
        tbl_9 = 0.05 * jax.random.normal(jax.random.fold_in(_tk, 500 + 9), (12500, 32), jnp.float32)
        tbl_10 = 0.05 * jax.random.normal(jax.random.fold_in(_tk, 500 + 10), (125000, 32), jnp.float32)
        tbl_11 = 0.05 * jax.random.normal(jax.random.fold_in(_tk, 500 + 11), (125000, 32), jnp.float32)
        tbl_12 = 0.05 * jax.random.normal(jax.random.fold_in(_tk, 500 + 12), (12500, 32), jnp.float32)
        tbl_13 = 0.05 * jax.random.normal(jax.random.fold_in(_tk, 500 + 13), (1000, 32), jnp.float32)
        tbl_14 = 0.05 * jax.random.normal(jax.random.fold_in(_tk, 500 + 14), (12500, 32), jnp.float32)
        tbl_15 = 0.05 * jax.random.normal(jax.random.fold_in(_tk, 500 + 15), (125000, 32), jnp.float32)
        tbl_16 = 0.05 * jax.random.normal(jax.random.fold_in(_tk, 500 + 16), (12500, 32), jnp.float32)
        tbl_17 = 0.05 * jax.random.normal(jax.random.fold_in(_tk, 500 + 17), (12500, 32), jnp.float32)
        tbl_18 = 0.05 * jax.random.normal(jax.random.fold_in(_tk, 500 + 18), (12500, 32), jnp.float32)
        tbl_19 = 0.05 * jax.random.normal(jax.random.fold_in(_tk, 500 + 19), (1250, 32), jnp.float32)
        tbl_20 = 0.05 * jax.random.normal(jax.random.fold_in(_tk, 500 + 20), (12500, 32), jnp.float32)
        tbl_21 = 0.05 * jax.random.normal(jax.random.fold_in(_tk, 500 + 21), (12500, 32), jnp.float32)
        tbl_22 = 0.05 * jax.random.normal(jax.random.fold_in(_tk, 500 + 22), (1250, 32), jnp.float32)
        tbl_23 = 0.05 * jax.random.normal(jax.random.fold_in(_tk, 500 + 23), (125000, 32), jnp.float32)
        tbl_24 = 0.05 * jax.random.normal(jax.random.fold_in(_tk, 500 + 24), (1000, 32), jnp.float32)
        tbl_25 = 0.05 * jax.random.normal(jax.random.fold_in(_tk, 500 + 25), (12500, 32), jnp.float32)
        tbl_26 = 0.05 * jax.random.normal(jax.random.fold_in(_tk, 500 + 26), (12500, 32), jnp.float32)
        tbl_27 = 0.05 * jax.random.normal(jax.random.fold_in(_tk, 500 + 27), (1000, 32), jnp.float32)
        tbl_28 = 0.05 * jax.random.normal(jax.random.fold_in(_tk, 500 + 28), (1000, 32), jnp.float32)
        tbl_29 = 0.05 * jax.random.normal(jax.random.fold_in(_tk, 500 + 29), (12500, 32), jnp.float32)
        tbl_30 = 0.05 * jax.random.normal(jax.random.fold_in(_tk, 500 + 30), (12500, 32), jnp.float32)
        tbl_31 = 0.05 * jax.random.normal(jax.random.fold_in(_tk, 500 + 31), (1000, 32), jnp.float32)
        tbl_32 = 0.05 * jax.random.normal(jax.random.fold_in(_tk, 500 + 32), (1000, 32), jnp.float32)
        tbl_33 = 0.05 * jax.random.normal(jax.random.fold_in(_tk, 500 + 33), (1000, 32), jnp.float32)
        tbl_34 = 0.05 * jax.random.normal(jax.random.fold_in(_tk, 500 + 34), (12500, 32), jnp.float32)
        tbl_35 = 0.05 * jax.random.normal(jax.random.fold_in(_tk, 500 + 35), (1250, 32), jnp.float32)
        tbl_36 = 0.05 * jax.random.normal(jax.random.fold_in(_tk, 500 + 36), (12500, 32), jnp.float32)
        tbl_37 = 0.05 * jax.random.normal(jax.random.fold_in(_tk, 500 + 37), (12500, 32), jnp.float32)
        tbl_38 = 0.05 * jax.random.normal(jax.random.fold_in(_tk, 500 + 38), (1250, 32), jnp.float32)
        _rk = jax.random.fold_in(_tk, 7)
        W_top1 = 0.0363456 * jax.random.normal(jax.random.fold_in(_tk, 801), (757, 512), jnp.float32)
        W_top2 = 0.0441942 * jax.random.normal(jax.random.fold_in(_tk, 802), (512, 256), jnp.float32)
        W_top3 = 0.0625 * jax.random.normal(jax.random.fold_in(_tk, 803), (256, 1), jnp.float32)
        b_top1 = jnp.zeros((512,), jnp.float32)
        b_top2 = jnp.zeros((256,), jnp.float32)
        return (dense_ctx, ids, tbl_0, tbl_1, tbl_2, tbl_3, tbl_4, tbl_5, tbl_6, tbl_7, tbl_8, tbl_9, tbl_10, tbl_11, tbl_12, tbl_13, tbl_14, tbl_15, tbl_16, tbl_17, tbl_18, tbl_19, tbl_20, tbl_21, tbl_22, tbl_23, tbl_24, tbl_25, tbl_26, tbl_27, tbl_28, tbl_29, tbl_30, tbl_31, tbl_32, tbl_33, tbl_34, tbl_35, tbl_36, tbl_37, tbl_38, W_top1, b_top1, W_top2, b_top2, W_top3)
    dense_ctx, ids, tbl_0, tbl_1, tbl_2, tbl_3, tbl_4, tbl_5, tbl_6, tbl_7, tbl_8, tbl_9, tbl_10, tbl_11, tbl_12, tbl_13, tbl_14, tbl_15, tbl_16, tbl_17, tbl_18, tbl_19, tbl_20, tbl_21, tbl_22, tbl_23, tbl_24, tbl_25, tbl_26, tbl_27, tbl_28, tbl_29, tbl_30, tbl_31, tbl_32, tbl_33, tbl_34, tbl_35, tbl_36, tbl_37, tbl_38, W_top1, b_top1, W_top2, b_top2, W_top3 = _rec_inputs()

    def _L0_rec_setup():
        import jax, jax.numpy as jnp
        import numpy as np
        F = 39

        def _pair_indices(f):
            row, col = ([], [])
            for i in range(f - 1):
                for j in range(i + 1, f):
                    row.append(i)
                    col.append(j)
            return (np.array(row, np.int32), np.array(col, np.int32))
        ROW, COL = _pair_indices(F)
        key = jax.random.key(seed)
        k1, k2 = jax.random.split(key)
        B, k = (1024, 32)
        P = F * (F - 1) // 2
        inputs = jax.random.normal(k1, (B, F, k), dtype=jnp.float32)
        w = jax.random.normal(k2, (k, P, k), dtype=jnp.float32)
        return {'inputs': inputs, 'w': w}
    _L0_rec_all = _L0_rec_setup()
    _L0_rec_in = {k: v for k, v in _L0_rec_all.items() if k in ('w',)}
    del _L0_rec_all
    return {'dense_ctx': dense_ctx, 'ids': ids, 'tbl_0': tbl_0, 'tbl_1': tbl_1, 'tbl_2': tbl_2, 'tbl_3': tbl_3, 'tbl_4': tbl_4, 'tbl_5': tbl_5, 'tbl_6': tbl_6, 'tbl_7': tbl_7, 'tbl_8': tbl_8, 'tbl_9': tbl_9, 'tbl_10': tbl_10, 'tbl_11': tbl_11, 'tbl_12': tbl_12, 'tbl_13': tbl_13, 'tbl_14': tbl_14, 'tbl_15': tbl_15, 'tbl_16': tbl_16, 'tbl_17': tbl_17, 'tbl_18': tbl_18, 'tbl_19': tbl_19, 'tbl_20': tbl_20, 'tbl_21': tbl_21, 'tbl_22': tbl_22, 'tbl_23': tbl_23, 'tbl_24': tbl_24, 'tbl_25': tbl_25, 'tbl_26': tbl_26, 'tbl_27': tbl_27, 'tbl_28': tbl_28, 'tbl_29': tbl_29, 'tbl_30': tbl_30, 'tbl_31': tbl_31, 'tbl_32': tbl_32, 'tbl_33': tbl_33, 'tbl_34': tbl_34, 'tbl_35': tbl_35, 'tbl_36': tbl_36, 'tbl_37': tbl_37, 'tbl_38': tbl_38, 'W_top1': W_top1, 'b_top1': b_top1, 'W_top2': W_top2, 'b_top2': b_top2, 'W_top3': W_top3, 'L0_rec_w': _L0_rec_in['w']}

def reference(dense_ctx, ids, tbl_0, tbl_1, tbl_2, tbl_3, tbl_4, tbl_5, tbl_6, tbl_7, tbl_8, tbl_9, tbl_10, tbl_11, tbl_12, tbl_13, tbl_14, tbl_15, tbl_16, tbl_17, tbl_18, tbl_19, tbl_20, tbl_21, tbl_22, tbl_23, tbl_24, tbl_25, tbl_26, tbl_27, tbl_28, tbl_29, tbl_30, tbl_31, tbl_32, tbl_33, tbl_34, tbl_35, tbl_36, tbl_37, tbl_38, W_top1, b_top1, W_top2, b_top2, W_top3, L0_rec_w):
    import jax
    import jax.numpy as jnp

    def _L0_rec_ref(inputs, w):
        import jax, jax.numpy as jnp
        import numpy as np
        F = 39

        def _pair_indices(f):
            row, col = ([], [])
            for i in range(f - 1):
                for j in range(i + 1, f):
                    row.append(i)
                    col.append(j)
            return (np.array(row, np.int32), np.array(col, np.int32))
        ROW, COL = _pair_indices(F)
        p = inputs[:, ROW, :]
        q = inputs[:, COL, :]
        return jnp.einsum('bpc,apc,bpa->bp', p, w, q)
    e = jnp.stack([tbl_0[ids[:, 0]], tbl_1[ids[:, 1]], tbl_2[ids[:, 2]], tbl_3[ids[:, 3]], tbl_4[ids[:, 4]], tbl_5[ids[:, 5]], tbl_6[ids[:, 6]], tbl_7[ids[:, 7]], tbl_8[ids[:, 8]], tbl_9[ids[:, 9]], tbl_10[ids[:, 10]], tbl_11[ids[:, 11]], tbl_12[ids[:, 12]], tbl_13[ids[:, 13]], tbl_14[ids[:, 14]], tbl_15[ids[:, 15]], tbl_16[ids[:, 16]], tbl_17[ids[:, 17]], tbl_18[ids[:, 18]], tbl_19[ids[:, 19]], tbl_20[ids[:, 20]], tbl_21[ids[:, 21]], tbl_22[ids[:, 22]], tbl_23[ids[:, 23]], tbl_24[ids[:, 24]], tbl_25[ids[:, 25]], tbl_26[ids[:, 26]], tbl_27[ids[:, 27]], tbl_28[ids[:, 28]], tbl_29[ids[:, 29]], tbl_30[ids[:, 30]], tbl_31[ids[:, 31]], tbl_32[ids[:, 32]], tbl_33[ids[:, 33]], tbl_34[ids[:, 34]], tbl_35[ids[:, 35]], tbl_36[ids[:, 36]], tbl_37[ids[:, 37]], tbl_38[ids[:, 38]]], axis=1)
    z = _L0_rec_ref(e, L0_rec_w)
    z = z.reshape(z.shape[0], -1)
    h = jnp.concatenate([z, dense_ctx], axis=1)
    h = jnp.maximum(h @ W_top1 + b_top1, 0.0)
    h = jnp.maximum(h @ W_top2 + b_top2, 0.0)
    y = h @ W_top3
    return y

_drawn_inputs = setup_inputs


def setup_inputs(seed=0):
    import zlib

    import numpy as np

    out = dict(_drawn_inputs(seed))
    spreads = {'b_top1': (0.0, 0.1), 'b_top2': (0.0, 0.1)}
    factors = {}
    for name, (base, spread) in spreads.items():
        noise = np.random.default_rng([zlib.crc32(name.encode()), seed]).standard_normal(out[name].shape)
        drawn = base * np.exp(spread * noise) if base else spread * noise
        out[name] = jnp.asarray(drawn.astype(out[name].dtype))
    for name, factor in factors.items():
        out[name] = (out[name] * factor).astype(out[name].dtype)
    return out
```

```python
import numpy as np
from contextlib import ExitStack

import concourse.bass as bass
import concourse.mybir as mybir

BATCH = 512
ITEMS = 39
DIM = 32
DENSE = 16
HIDDEN1 = 512
HIDDEN2 = 256
LANES = 128
QUAD = 4
BATCH_TILES = BATCH // LANES
BLOCKS = -(-ITEMS // QUAD)
LAST_BLOCK = BLOCKS - 1
LAST = ITEMS - 1
CHUNK_TILES = 16
STAGED = CHUNK_TILES // QUAD
WINDOW = 2 * DIM + QUAD
M1 = HIDDEN1 // LANES
M2 = HIDDEN2 // LANES


def pair_index(i, j):
    return i * (2 * ITEMS - i - 1) // 2 + j - i - 1


def plan_tiles():
    tiles = []
    for j in range(ITEMS):
        tiles += [(j, n, QUAD) for n in range(j // QUAD)]
        if j % QUAD == QUAD - 1:
            tiles += [(j - QUAD + 1 + k, j // QUAD, k) for k in range(1, QUAD)]
        elif j // QUAD == LAST_BLOCK and j % QUAD:
            tiles.append((j, LAST_BLOCK, j % QUAD))
    return [t for k in range(0, len(tiles), 2) for t in sorted(tiles[k:k + 2], key=lambda t: t[1])]


def plan_rows(tiles):
    rows = []
    chunk, used = 0, [0, 0, 0, DENSE]
    for k in range(0, len(tiles), QUAD):
        sizes = [t[2] for t in tiles[k:k + QUAD]]
        order = sorted(range(QUAD), key=lambda t: -sizes[t])
        groups = sorted(range(QUAD), key=lambda g: used[g])
        if any(used[g] + sizes[t] > DIM for t, g in zip(order, groups)):
            chunk, used = chunk + 1, [0] * QUAD
            groups = list(range(QUAD))
        place = dict(zip(order, groups))
        for t in range(QUAD):
            g = place[t]
            start = used[g] - (DENSE if chunk == 0 and g == QUAD - 1 else 0)
            rows.append((chunk, g, start))
            used[g] += sizes[t]
    return rows


TILES = plan_tiles()
ROWS = plan_rows(TILES)
N_TILES = len(TILES)
UNITS = N_TILES // 2
ROUNDS = N_TILES // QUAD
W_CHUNKS = -(-N_TILES // CHUNK_TILES)
CHUNK_UNITS = CHUNK_TILES // 2
CHUNK_ROUNDS = CHUNK_TILES // QUAD
W_SLOTS = 3
Z_CHUNKS = ROWS[-1][0] + 1
DENSE_ROW = LANES - DENSE
PRODUCT_SLOTS = 4
SPLIT_SLOTS = 4


def first_round(wanted):
    return min(k for k, t in enumerate(TILES) if wanted(*t)) // QUAD


def plan_turns():
    turns = [[] for _ in range(ROUNDS)]
    for j in range(1, ITEMS):
        turns[max(first_round(lambda i, n, k: i == j) - 1, 0)].append(("item", j))
        if j % QUAD == QUAD - 1 or j == LAST - 1:
            n = j // QUAD
            turns[max(first_round(lambda i, m, k: m == n) - 1, 0)].append(("block", n))
    return turns


TURNS = plan_turns()
TURN_ORDER = [t for turns in TURNS for t in turns]
TURN_INDEX = {t: k for k, t in enumerate(TURN_ORDER)}
LAST_TURN_ROUND = max(r for r in range(ROUNDS) if TURNS[r])
Z_LAST_ROUND = [max(k for k in range(N_TILES) if ROWS[k][0] == c) // QUAD for c in range(Z_CHUNKS)]


def build(nc, dense_t, ids, tables, w_tiles, w1, b1, w2, b2, w3, identity, summing, out):
    f32 = mybir.dt.float32
    f32r = mybir.dt.float32r
    ALU = mybir.AluOpType
    ACT = mybir.ActivationFunctionType

    with ExitStack() as stack:
        def sbuf(name, shape, dtype=f32):
            return stack.enter_context(nc.sbuf_tensor(name, shape, dtype))

        def psum(name, shape):
            return stack.enter_context(nc.psum_tensor(name, shape, f32))

        def sem(name):
            return stack.enter_context(nc.semaphore(name))

        ids_sb = sbuf("ids_sb", [LANES, BATCH_TILES, ITEMS], mybir.dt.int32)
        identity_sb = sbuf("identity_sb", [LANES, LANES])
        summing_sb = sbuf("summing_sb", [LANES, WINDOW])
        rows_sb = sbuf("rows_sb", [LANES, BLOCKS, BATCH_TILES, QUAD, DIM])
        split_sb = sbuf("split_sb", [LANES, SPLIT_SLOTS, BATCH_TILES, 2, 2, DIM], f32r)
        stack_sb = sbuf("stack_sb", [LANES, ITEMS - 1, BATCH], f32r)
        block_sb = sbuf("block_sb", [LANES, BLOCKS, BATCH])
        w_raw = sbuf("w_raw", [LANES, 2, STAGED * LANES])
        w_head = sbuf("w_head", [LANES, STAGED * LANES], f32r)
        w_rest = sbuf("w_rest", [LANES, STAGED * LANES], f32r)
        w_sb = sbuf("w_sb", [LANES, W_SLOTS, CHUNK_TILES, LANES], f32r)
        product_sb = sbuf("product_sb", [LANES, PRODUCT_SLOTS, 2, BATCH])
        z_sb = sbuf("z_sb", [LANES, Z_CHUNKS, BATCH])
        w1_sb = sbuf("w1_sb", [LANES, Z_CHUNKS, HIDDEN1])
        w2_sb = sbuf("w2_sb", [LANES, M1, HIDDEN2])
        w3_sb = sbuf("w3_sb", [LANES, M2])
        b1_sb = sbuf("b1_sb", [LANES, M1])
        b2_sb = sbuf("b2_sb", [LANES, M2])
        y_sb = sbuf("y_sb", [1, BATCH])
        rows_flat = rows_sb[:].rearrange("p n t q d -> p (n t q d)")
        hidden1_sb = rows_flat[:, 0:M1 * BATCH].rearrange("p (m b) -> p m b", m=M1)
        hidden2_sb = rows_flat[:, M1 * BATCH:(M1 + M2) * BATCH].rearrange("p (m b) -> p m b", m=M2)

        u_ps = psum("u_ps", [LANES, 4, BATCH])
        z_ps = psum("z_ps", [LANES, BATCH])
        turn_ps = psum("turn_ps", [LANES, 2, BATCH])
        hidden_ps = psum("hidden_ps", [LANES, BATCH])
        hidden1_ps = [hidden_ps[:], turn_ps[:, 0, :], turn_ps[:, 1, :], u_ps[:, 0, :]]
        hidden2_ps = [u_ps[:, 2, :], u_ps[:, 3, :]]
        y_ps = u_ps[0:1, 1, :]

        ids_loaded = sem("ids_loaded")
        constants_loaded = sem("constants_loaded")
        tail_loaded = sem("tail_loaded")
        gathered = [sem(f"gathered_{j}") for j in range(ITEMS)]
        heads_cut = sem("heads_cut")
        rests_cut = sem("rests_cut")
        turned = sem("turned")
        lifted = sem("lifted")
        w_loaded = [sem(f"w_loaded_{s}") for s in range(2)]
        w_heads_cut = sem("w_heads_cut")
        w_rests_cut = sem("w_rests_cut")
        w_spread = [sem(f"w_spread_{s}") for s in range(W_SLOTS)]
        u_made = sem("u_made")
        multiplied = sem("multiplied")
        summed = sem("summed")
        z_kept = sem("z_kept")
        last_block_cleared = sem("last_block_cleared")
        hidden1_made = sem("hidden1_made")
        hidden1_kept = sem("hidden1_kept")
        hidden2_made = sem("hidden2_made")
        hidden2_kept = sem("hidden2_kept")
        y_made = sem("y_made")
        y_kept = sem("y_kept")
        stored = sem("stored")
        TAIL_LOADS = 6 * 16

        block = stack.enter_context(nc.Block())

        def rounds_of(chunk):
            return max(CHUNK_ROUNDS * (chunk - W_SLOTS + 1), 0)

        W_SPLITS = [[c for c in range(W_CHUNKS) if rounds_of(c) == r] for r in range(ROUNDS)]

        def item_rows(j):
            rows = rows_sb[:, j // QUAD, :, j % QUAD, :]
            return rows.unsqueeze(2).broadcast_to([LANES, BATCH_TILES, 2, DIM])

        @block.gpsimd
        def _(pool):
            pool.wait_ge(ids_loaded, 16)
            for j in range(ITEMS):
                for t in range(BATCH_TILES):
                    pool.indirect_dma_start(
                        rows_sb[:, j // QUAD, t, j % QUAD, :], None, tables[j],
                        bass.IndirectOffsetOnAxis(ap=ids_sb[:, t, j:j + 1], axis=0),
                    ).then_inc(gathered[j], 16)

        @block.sync
        def _(sp):
            sp.dma_start(ids_sb[:], ids.rearrange("(t p) f -> p t f", p=LANES)).then_inc(ids_loaded, 16)
            for c in range(2):
                sp.dma_start(w_raw[:, c, :], w_tiles[c]).then_inc(w_loaded[c], 16)
            sp.dma_start(identity_sb[:], identity).then_inc(constants_loaded, 16)
            sp.dma_start(summing_sb[:], summing).then_inc(constants_loaded, 16)
            for c in range(W_CHUNKS):
                sp.wait_ge(w_heads_cut, c + 1)
                sp.wait_ge(w_rests_cut, c + 1)
                if c >= W_SLOTS:
                    sp.wait_ge(u_made, CHUNK_UNITS * (c - W_SLOTS + 1))
                for copy in range(QUAD):
                    part = w_head if copy < 2 else w_rest
                    for g in range(QUAD):
                        sp.dma_start(
                            w_sb[DIM * copy:DIM * (copy + 1), c % W_SLOTS,
                                 STAGED * g:STAGED * (g + 1), :].bitcast(f32),
                            part[DIM * g:DIM * (g + 1), :].rearrange("p (t m) -> p t m", m=LANES).bitcast(f32),
                        ).then_inc(w_spread[c % W_SLOTS], 16)
                if c + 2 < W_CHUNKS:
                    sp.dma_start(w_raw[:, c % 2, :], w_tiles[c + 2]).then_inc(w_loaded[c % 2], 16)
                if c == 1:
                    sp.dma_start(w1_sb[:], w1.rearrange("c p n -> p c n")).then_inc(tail_loaded, 16)
                    sp.dma_start(w2_sb[:], w2.rearrange("(m p) n -> p m n", p=LANES)).then_inc(tail_loaded, 16)
                    sp.dma_start(w3_sb[:], w3).then_inc(tail_loaded, 16)
                    sp.dma_start(b1_sb[:], b1).then_inc(tail_loaded, 16)
                    sp.dma_start(b2_sb[:], b2).then_inc(tail_loaded, 16)
                    sp.dma_start(z_sb[DENSE_ROW:LANES, 0, :], dense_t).then_inc(tail_loaded, 16)
            sp.wait_ge(y_kept, 1)
            sp.dma_start(out, y_sb[:]).then_inc(stored, 16)
            sp.wait_ge(stored, 16)

        @block.scalar
        def _(act):
            def cut_w_heads(c):
                act.wait_ge(w_loaded[c % 2], 16 * (c // 2 + 1))
                if c:
                    act.wait_ge(w_spread[(c - 1) % W_SLOTS], 256 * ((c - 1) // W_SLOTS + 1))
                act.activation(w_head[:], w_raw[:, c % 2, :], ACT.Copy).then_inc(w_heads_cut, 1)

            def cut_item_head(j):
                act.wait_ge(gathered[j], 16 * BATCH_TILES)
                if j > SPLIT_SLOTS:
                    act.wait_ge(turned, TURN_INDEX["item", j - SPLIT_SLOTS] + 1)
                act.activation(split_sb[:, j % SPLIT_SLOTS, :, :, 0, :], item_rows(j), ACT.Copy).then_inc(heads_cut, 1)

            def lift(turn):
                act.wait_ge(turned, TURN_INDEX[turn] + 1)
                source = turn_ps[:, TURN_INDEX[turn] % 2, :]
                kind, k = turn
                if kind == "item":
                    act.activation(stack_sb[:, k - 1, :], source, ACT.Copy).then_inc(lifted, 1)
                elif k < LAST_BLOCK:
                    act.activation(block_sb[:, k, :], source, ACT.Copy).then_inc(lifted, 1)
                else:
                    act.wait_ge(last_block_cleared, 1)
                    act.activation(block_sb[0:2 * DIM, k, :], source[0:2 * DIM, :],
                                   ACT.Copy).then_inc(lifted, 1)

            def keep_z(c):
                act.wait_ge(summed, Z_LAST_ROUND[c] + 1)
                lanes = DENSE_ROW if c == 0 else LANES
                act.activation(z_sb[0:lanes, c, :], z_ps[0:lanes, :], ACT.Copy).then_inc(z_kept, 1)

            for r in range(ROUNDS):
                for c in W_SPLITS[r]:
                    cut_w_heads(c)
                for turn in TURNS[r]:
                    if turn[0] == "item":
                        cut_item_head(turn[1])
                    lift(turn)
                for c in range(Z_CHUNKS):
                    if Z_LAST_ROUND[c] == r - 1:
                        keep_z(c)
            for c in range(Z_CHUNKS):
                if Z_LAST_ROUND[c] == ROUNDS - 1:
                    keep_z(c)
            act.wait_ge(tail_loaded, TAIL_LOADS)
            for m in range(M1):
                act.wait_ge(hidden1_made, m + 1)
                act.activation(hidden1_sb[:, m, :], hidden1_ps[m], ACT.Relu,
                               bias=b1_sb[:, m:m + 1]).then_inc(hidden1_kept, 1)
            for m in range(M2):
                act.wait_ge(hidden2_made, m + 1)
                act.activation(hidden2_sb[:, m, :], hidden2_ps[m], ACT.Relu,
                               bias=b2_sb[:, m:m + 1]).then_inc(hidden2_kept, 1)
            act.wait_ge(y_made, 1)
            act.activation(y_sb[:], y_ps, ACT.Copy).then_inc(y_kept, 1)

        @block.vector
        def _(dve):
            dve.memset(block_sb[2 * DIM:LANES, LAST_BLOCK, :], 0.0).then_inc(last_block_cleared, 1)

            def cut_w_rests(c):
                dve.wait_ge(w_heads_cut, c + 1)
                dve.tensor_tensor(w_rest[:], w_raw[:, c % 2, :], w_head[:].bitcast(f32),
                                  ALU.subtract).then_inc(w_rests_cut, 1)

            def cut_item_rest(j):
                dve.wait_ge(heads_cut, j)
                slot = split_sb[:, j % SPLIT_SLOTS]
                dve.tensor_tensor(slot[:, :, :, 1, :], item_rows(j), slot[:, :, :, 0, :].bitcast(f32),
                                  ALU.subtract).then_inc(rests_cut, 1)

            for r in range(ROUNDS):
                for c in W_SPLITS[r]:
                    cut_w_rests(c)
                for kind, k in TURNS[r]:
                    if kind == "item":
                        cut_item_rest(k)
                for k in (2 * r, 2 * r + 1):
                    low, high = TILES[2 * k][1], TILES[2 * k + 1][1]
                    if low == high:
                        factor = block_sb[:, low:low + 1, :].broadcast_to([LANES, 2, BATCH])
                    else:
                        factor = block_sb[:, low:high + 1:high - low, :]
                    dve.wait_ge(u_made, k + 1)
                    dve.wait_ge(lifted, max(TURN_INDEX["block", n] for n in (low, high)) + 1)
                    if k >= PRODUCT_SLOTS:
                        dve.wait_ge(summed, (k - PRODUCT_SLOTS) // 2 + 1)
                    half = 2 * (k % 2)
                    dve.tensor_tensor(product_sb[:, k % PRODUCT_SLOTS, :, :], u_ps[:, half:half + 2, :],
                                      factor, ALU.mult).then_inc(multiplied, 1)

        @block.tensor
        def _(pe):
            def turn(what):
                kind, k = what
                use = TURN_INDEX[what]
                bank = turn_ps[:, use % 2, :]
                if use >= 2:
                    pe.wait_ge(lifted, use - 1)
                if kind == "item":
                    pe.wait_ge(rests_cut, k)
                else:
                    for j in range(QUAD * k, min(QUAD * (k + 1), LAST)):
                        pe.wait_ge(gathered[j], 16 * BATCH_TILES)
                for t in range(BATCH_TILES):
                    if kind == "item":
                        source = split_sb[:, k % SPLIT_SLOTS, t].rearrange("p c h d -> p (c h d)").bitcast(f32)
                        lanes = LANES
                    else:
                        items = QUAD if k < LAST_BLOCK else 2
                        lanes = items * DIM
                        source = rows_sb[:, k, t, 0:items, :].rearrange("p q d -> p (q d)")
                    last = nc.tensor.transpose(bank[0:lanes, LANES * t:LANES * (t + 1)], source, identity_sb[:])
                last.then_inc(turned, 1)

            def contract(k):
                if k % CHUNK_UNITS == 0:
                    c = k // CHUNK_UNITS
                    pe.wait_ge(w_spread[c % W_SLOTS], 256 * (c // W_SLOTS + 1))
                if k >= 2:
                    pe.wait_ge(multiplied, k - 1)
                pe.wait_ge(lifted, max(TURN_INDEX["item", TILES[s][0]] for s in (2 * k, 2 * k + 1)) + 1)
                for s in (2 * k, 2 * k + 1):
                    c = s // CHUNK_TILES
                    last = nc.tensor.matmul(u_ps[:, s % 4, :], w_sb[:, c % W_SLOTS, s % CHUNK_TILES, :],
                                            stack_sb[:, TILES[s][0] - 1, :], start=True, stop=True)
                last.then_inc(u_made, 1)

            begun = set()

            def add_up(r):
                pe.wait_ge(multiplied, 2 * r + 2)
                for s in range(QUAD * r, QUAD * (r + 1)):
                    chunk, group, row = ROWS[s]
                    if chunk and chunk not in [x[0] for x in begun]:
                        pe.wait_ge(z_kept, chunk)
                    first = (chunk, group) not in begun
                    begun.add((chunk, group))
                    final = s == max(x for x in range(N_TILES) if ROWS[x][:2] == (chunk, group))
                    last = nc.tensor.matmul(
                        z_ps[DIM * group:DIM * (group + 1), :],
                        summing_sb[:, DIM - row:2 * DIM - row],
                        product_sb[:, (s // 2) % PRODUCT_SLOTS, s % 2, :],
                        start=first, stop=final, tile_position=(0, DIM * group))
                last.then_inc(summed, 1)

            def layer1(m, c):
                pe.wait_ge(z_kept, c + 1)
                last = nc.tensor.matmul(hidden1_ps[m], w1_sb[:, c, LANES * m:LANES * (m + 1)], z_sb[:, c, :],
                                        start=c == 0, stop=c == Z_CHUNKS - 1)
                if c == Z_CHUNKS - 1:
                    last.then_inc(hidden1_made, 1)

            pe.wait_ge(constants_loaded, 32)
            for r in range(ROUNDS):
                for what in TURNS[r]:
                    turn(what)
                contract(2 * r)
                contract(2 * r + 1)
                if r:
                    add_up(r - 1)
                for c in range(Z_CHUNKS):
                    if Z_LAST_ROUND[c] == r - 3:
                        if c == 0:
                            pe.wait_ge(tail_loaded, TAIL_LOADS)
                        layer1(0, c)
            pe.wait_ge(lifted, len(TURN_ORDER))
            for c in range(Z_CHUNKS - 1):
                layer1(1, c)
            add_up(ROUNDS - 1)
            for c in range(Z_CHUNKS - 1):
                layer1(2, c)
            for c in range(Z_CHUNKS - 1):
                layer1(3, c)
            for m in range(M1):
                layer1(m, Z_CHUNKS - 1)
            for m in range(M1):
                pe.wait_ge(hidden1_kept, m + 1)
                for n in range(M2):
                    last = nc.tensor.matmul(hidden2_ps[n], w2_sb[:, m, LANES * n:LANES * (n + 1)],
                                            hidden1_sb[:, m, :], start=m == 0, stop=m == M1 - 1)
                    if m == M1 - 1:
                        last.then_inc(hidden2_made, 1)
            for n in range(M2):
                pe.wait_ge(hidden2_kept, n + 1)
                last = nc.tensor.matmul(y_ps, w3_sb[:, n:n + 1], hidden2_sb[:, n, :],
                                        start=n == 0, stop=n == M2 - 1)
            last.then_inc(y_made, 1)


def lay_out_w(w):
    flat = np.zeros((DIM, W_CHUNKS * CHUNK_TILES, QUAD, DIM), w.dtype)
    for s, (j, n, pairs) in enumerate(TILES):
        for q in range(pairs):
            flat[:, s, q, :] = w[:, pair_index(QUAD * n + q, j), :]
    flat = flat.reshape(DIM, W_CHUNKS, QUAD, STAGED * LANES)
    return np.ascontiguousarray(flat.transpose(1, 2, 0, 3).reshape(W_CHUNKS, LANES, STAGED * LANES))


def lay_out_w1(w1):
    rows = np.zeros((Z_CHUNKS, LANES, HIDDEN1), w1.dtype)
    for s, (j, n, pairs) in enumerate(TILES):
        chunk, group, row = ROWS[s]
        for q in range(pairs):
            rows[chunk, DIM * group + row + q] = w1[pair_index(QUAD * n + q, j)]
    rows[0, DENSE_ROW:] = w1[ITEMS * (ITEMS - 1) // 2:]
    return rows


def kernel(**inputs):
    import concourse.bacc as bacc
    from concourse.bass_utils import run_bass_kernel_spmd

    given = {k: np.asarray(v) for k, v in inputs.items()}
    summing = np.zeros((LANES, WINDOW), np.float32)
    for q in range(QUAD):
        summing[DIM * q:DIM * (q + 1), DIM + q] = 1.0
    arrays = {
        "dense_t": np.ascontiguousarray(given["dense_ctx"].T),
        "ids": given["ids"],
        "w_tiles": lay_out_w(given["L0_rec_w"]),
        "w1": lay_out_w1(given["W_top1"]),
        "b1": np.ascontiguousarray(given["b_top1"].reshape(M1, LANES).T),
        "w2": given["W_top2"],
        "b2": np.ascontiguousarray(given["b_top2"].reshape(M2, LANES).T),
        "w3": np.ascontiguousarray(given["W_top3"].reshape(M2, LANES).T),
        "identity": np.eye(LANES, dtype=np.float32),
        "summing": summing,
    }
    arrays.update({f"tbl_{j}": given[f"tbl_{j}"] for j in range(ITEMS)})

    nc = bacc.Bacc("TRN2", target_bir_lowering=False, num_devices=1)
    aps = {name: nc.dram_tensor(f"in_{name}", a.shape, mybir.dt.from_np(a.dtype), kind="ExternalInput").ap()
           for name, a in arrays.items()}
    out = nc.dram_tensor("out_y", (1, BATCH), mybir.dt.float32, kind="ExternalOutput").ap()
    tables = [aps.pop(f"tbl_{j}") for j in range(ITEMS)]
    build(nc, tables=tables, out=out, **aps)
    run = run_bass_kernel_spmd(nc, [{f"in_{name}": a for name, a in arrays.items()}], core_ids=[0])
    return run.results[0]["out_y"].reshape(BATCH, 1)
```

```python
import numpy as np
from contextlib import ExitStack

import concourse.bass as bass
import concourse.mybir as mybir

BATCH = 512
ITEMS = 39
DIM = 32
DENSE = 16
HIDDEN1 = 512
HIDDEN2 = 256
LANES = 128
QUAD = 4
BATCH_TILES = BATCH // LANES
BLOCKS = -(-ITEMS // QUAD)
LAST_BLOCK = BLOCKS - 1
LAST = ITEMS - 1
CHUNK_TILES = 16
STAGED = CHUNK_TILES // QUAD
WINDOW = 2 * DIM + QUAD
M1 = HIDDEN1 // LANES
M2 = HIDDEN2 // LANES


def pair_index(i, j):
    return i * (2 * ITEMS - i - 1) // 2 + j - i - 1


def mixed_of(n):
    return n // 2 if n < LAST_BLOCK else LAST_BLOCK // 2


def plan_tiles():
    lower_inside = [(3, {1: 1, 2: 2}), (0, {3: 3}), (1, {0: 0})]
    lower_mixed = (2, {0: 0, 1: 1})
    upper_inside = [(1, {0: 0, 3: 3}), (2, {1: 1}), (3, {2: 2})]
    upper_mixed = (0, {2: 2, 3: 3})

    def moved(n, one):
        return QUAD * n + one[0], {q: QUAD * n + i for q, i in one[1].items()}

    tiles = []
    for j in range(ITEMS):
        n = j // QUAD
        tiles += [(("block", b), [(j, {q: QUAD * b + q for q in range(QUAD)})]) for b in range(n)]
        if j % QUAD == QUAD - 1:
            upper = n % 2 or n == LAST_BLOCK - 1
            inside = upper_inside if upper else lower_inside
            tiles.append((("block", n), [moved(n, one) for one in inside]))
            if n % 2:
                tiles.append((("mixed", mixed_of(n)), [moved(n - 1, lower_mixed), moved(n, upper_mixed)]))
        elif j == LAST - 1:
            tiles.append((("mixed", mixed_of(n)), [moved(n, (1, {0: 0})), moved(n - 1, upper_mixed)]))
        elif j == LAST:
            tiles.append((("block", n), [moved(n, lower_mixed)]))
    return [t for k in range(0, len(tiles), 2) for t in sorted(tiles[k:k + 2], key=lambda t: factor_slot(t[0]))]


def factor_slot(factor):
    kind, k = factor
    return k if kind == "block" else BLOCKS + k % MIXED_SLOTS


MIXED_SLOTS = 2
MIXED = mixed_of(LAST_BLOCK) + 1
TILES = plan_tiles()
N_TILES = len(TILES)
PASSES = [(s, j, pairs) for s, (factor, passes) in enumerate(TILES) for j, pairs in passes]
UNITS = N_TILES // 2
ROUNDS = -(-N_TILES // QUAD)
W_CHUNKS = -(-len(PASSES) // CHUNK_TILES)
W_SLOTS = 2
CHUNK_ROUNDS = DIM // QUAD
Z_CHUNKS = -(-ROUNDS // CHUNK_ROUNDS)
Z_LAST_ROUND = [min(CHUNK_ROUNDS * (c + 1), ROUNDS) - 1 for c in range(Z_CHUNKS)]
DENSE_HALF = DENSE // 2
DENSE_ROW = DIM - DENSE_HALF
assert N_TILES % QUAD == 2 and QUAD * (ROUNDS - 1) <= DIM * (Z_CHUNKS - 1) + DENSE_ROW
PRODUCT_SLOTS = 4
SPLIT_SLOTS = 3
SPLITS_PER_PAIR = 4
assert {tuple(sorted((i, j))) for s, j, pairs in PASSES for i in pairs.values()} == {
    (i, j) for j in range(ITEMS) for i in range(j)}


def units_before(c):
    return PASSES[min(CHUNK_TILES * (c + 1), len(PASSES)) - 1][0] // 2 + 1


def z_place(s):
    r = s // QUAD
    return r // CHUNK_ROUNDS, s % QUAD, QUAD * (r % CHUNK_ROUNDS)


def first_round(wanted):
    return min(s for s, t in enumerate(TILES) if wanted(t)) // QUAD


def plan_turns():
    early, late = [[] for _ in range(ROUNDS)], [[] for _ in range(ROUNDS)]
    pairs = [(j, j + 1) for j in range(0, LAST - 2, 2)] + [(LAST - 2,), (LAST - 1,), (LAST,)]
    for pair in pairs:
        use = first_round(lambda t: any(j in pair for j, _ in t[1]))
        early[max(use - 1, 0)].append(("items", pair))
    for n in range(BLOCKS):
        use = first_round(lambda t: t[0] == ("block", n) or t[0] == ("mixed", mixed_of(n)) and n * QUAD in
                          [i - i % QUAD for _, p in t[1] for i in p.values()])
        late[max(use - 1, 0)].append(("block", n))
    return early, late


EARLY_TURNS, LATE_TURNS = plan_turns()
TURN_ORDER = [t for r in range(ROUNDS) for t in EARLY_TURNS[r] + LATE_TURNS[r]]
TURN_INDEX = {t: k for k, t in enumerate(TURN_ORDER)}
ITEM_TURN = {j: TURN_INDEX[t] for t in TURN_ORDER if t[0] == "items" for j in t[1]}
ITEM_PAIRS = [t[1] for t in TURN_ORDER if t[0] == "items"]
LAST_TURN_ROUND = max(r for r in range(ROUNDS) if EARLY_TURNS[r] or LATE_TURNS[r])
MIXED_UNIT = {t[0][1]: s // 2 for s, t in enumerate(TILES) if t[0][0] == "mixed"}

if __name__ == "__main__":
    print(N_TILES, len(PASSES), UNITS, ROUNDS, W_CHUNKS, Z_CHUNKS, Z_LAST_ROUND)
    for r in range(ROUNDS):
        print(r, EARLY_TURNS[r], LATE_TURNS[r], [t[0] for t in TILES[QUAD*r:QUAD*r+QUAD]], [t[1][0][0] for t in TILES[QUAD*r:QUAD*r+QUAD]])


def build(nc, dense_t, ids, tables, w_tiles, w1, b1, w2, b2, w3, identity, summing, placing, out):
    f32 = mybir.dt.float32
    f32r = mybir.dt.float32r
    ALU = mybir.AluOpType
    ACT = mybir.ActivationFunctionType

    with ExitStack() as stack:
        def sbuf(name, shape, dtype=f32):
            return stack.enter_context(nc.sbuf_tensor(name, shape, dtype))

        def psum(name, shape):
            return stack.enter_context(nc.psum_tensor(name, shape, f32))

        def sem(name):
            return stack.enter_context(nc.semaphore(name))

        ids_sb = sbuf("ids_sb", [LANES, BATCH_TILES, ITEMS], mybir.dt.int32)
        identity_sb = sbuf("identity_sb", [LANES, LANES])
        identity_r = sbuf("identity_r", [LANES, LANES], f32r)
        summing_sb = sbuf("summing_sb", [LANES, WINDOW])
        placing_sb = sbuf("placing_sb", [DENSE, 2, DIM])
        dense_sb = sbuf("dense_sb", [DENSE, BATCH])
        rows_sb = sbuf("rows_sb", [LANES, BLOCKS, BATCH_TILES, QUAD, DIM])
        split_sb = sbuf("split_sb", [LANES, SPLIT_SLOTS, BATCH_TILES, 2, 2, DIM], f32r)
        stack_sb = sbuf("stack_sb", [LANES, ITEMS, BATCH], f32r)
        factor_sb = sbuf("factor_sb", [LANES, BLOCKS + MIXED_SLOTS, BATCH])
        w_raw = sbuf("w_raw", [LANES, 2, STAGED * LANES])
        w_head = sbuf("w_head", [LANES, 2, STAGED * LANES], f32r)
        w_rest = sbuf("w_rest", [LANES, 2, STAGED * LANES], f32r)
        w_parts = nc.dram_tensor("w_parts", (2, W_CHUNKS, LANES, STAGED * LANES), f32).ap()
        w_sb = sbuf("w_sb", [LANES, W_SLOTS, CHUNK_TILES, LANES], f32r)
        product_sb = sbuf("product_sb", [LANES, PRODUCT_SLOTS, 2, BATCH])
        z_sb = sbuf("z_sb", [LANES, Z_CHUNKS, BATCH])
        w1_sb = sbuf("w1_sb", [LANES, Z_CHUNKS, HIDDEN1])
        w2_sb = sbuf("w2_sb", [LANES, M1, HIDDEN2])
        w3_sb = sbuf("w3_sb", [LANES, M2])
        b1_sb = sbuf("b1_sb", [LANES, M1])
        b2_sb = sbuf("b2_sb", [LANES, M2])
        y_sb = sbuf("y_sb", [1, BATCH])
        rows_flat = rows_sb[:].rearrange("p n t q d -> p (n t q d)")
        hidden1_sb = rows_flat[:, 0:M1 * BATCH].rearrange("p (m b) -> p m b", m=M1)
        hidden2_sb = rows_flat[:, M1 * BATCH:(M1 + M2) * BATCH].rearrange("p (m b) -> p m b", m=M2)

        u_ps = psum("u_ps", [LANES, 4, BATCH])
        z_ps = psum("z_ps", [LANES, BATCH])
        turn_ps = psum("turn_ps", [LANES, BATCH])
        hidden_ps = psum("hidden_ps", [LANES, 2, BATCH])
        ending = 2 * ((UNITS - 1) % 2)
        free = 2 - ending
        hidden1_ps = [hidden_ps[:, 0, :], hidden_ps[:, 1, :], turn_ps[:], u_ps[:, free, :]]
        hidden2_ps = [u_ps[:, free + 1, :], u_ps[:, ending, :]]
        y_ps = u_ps[0:1, ending + 1, :]

        ids_loaded = sem("ids_loaded")
        constants_loaded = sem("constants_loaded")
        identity_rounded = sem("identity_rounded")
        tail_loaded = sem("tail_loaded")
        gathered = [sem(f"gathered_{j}") for j in range(ITEMS)]
        heads_cut = sem("heads_cut")
        rests_cut = sem("rests_cut")
        turned = sem("turned")
        lifted = sem("lifted")
        mixed_made = sem("mixed_made")
        w_loaded = [sem(f"w_loaded_{s}") for s in range(2)]
        w_heads_cut = sem("w_heads_cut")
        w_rests_cut = sem("w_rests_cut")
        w_stored = [sem(f"w_stored_{s}") for s in range(2)]
        w_spread = [sem(f"w_spread_{s}") for s in range(W_SLOTS)]
        u_made = sem("u_made")
        multiplied = sem("multiplied")
        summed = sem("summed")
        z_kept = sem("z_kept")
        last_block_cleared = sem("last_block_cleared")
        hidden1_made = sem("hidden1_made")
        hidden1_kept = sem("hidden1_kept")
        hidden2_made = sem("hidden2_made")
        hidden2_kept = sem("hidden2_kept")
        y_made = sem("y_made")
        y_kept = sem("y_kept")
        stored = sem("stored")
        TAIL_LOADS = 7 * 16

        block = stack.enter_context(nc.Block())

        def w_chunks_before(turn):
            p = ITEM_PAIRS.index(turn[1])
            first = W_SLOTS + SPLITS_PER_PAIR * (p - 1)
            return range(min(first, W_CHUNKS) if p else 0, min(first + SPLITS_PER_PAIR, W_CHUNKS))

        def item_rows(j):
            return rows_sb[:, j // QUAD, :, j % QUAD, :]

        @block.gpsimd
        def _(pool):
            pool.wait_ge(ids_loaded, 16)
            for j in range(ITEMS):
                for t in range(BATCH_TILES):
                    pool.indirect_dma_start(
                        rows_sb[:, j // QUAD, t, j % QUAD, :], None, tables[j],
                        bass.IndirectOffsetOnAxis(ap=ids_sb[:, t, j:j + 1], axis=0),
                    ).then_inc(gathered[j], 16)

        @block.sync
        def _(sp):
            sp.dma_start(ids_sb[:], ids.rearrange("(t p) f -> p t f", p=LANES)).then_inc(ids_loaded, 16)
            for c in range(2):
                sp.dma_start(w_raw[:, c, :], w_tiles[c]).then_inc(w_loaded[c], 16)
            sp.dma_start(identity_sb[:], identity).then_inc(constants_loaded, 16)
            sp.dma_start(summing_sb[:], summing).then_inc(constants_loaded, 16)

            def store_parts(c):
                sp.wait_ge(w_heads_cut, c + 1)
                sp.dma_start(w_parts[0, c], w_head[:, c % 2, :].bitcast(f32)).then_inc(w_stored[c % 2], 16)
                sp.wait_ge(w_rests_cut, c + 1)
                sp.dma_start(w_parts[1, c], w_rest[:, c % 2, :].bitcast(f32)).then_inc(w_stored[c % 2], 16)
                if c + 2 < W_CHUNKS:
                    sp.dma_start(w_raw[:, c % 2, :], w_tiles[c + 2]).then_inc(w_loaded[c % 2], 16)

            def spread(c):
                sp.wait_ge(w_stored[c % 2], 32 * (c // 2 + 1))
                if c >= W_SLOTS:
                    sp.wait_ge(u_made, units_before(c - W_SLOTS))
                for copy in range(QUAD):
                    sp.dma_start(
                        w_sb[DIM * copy:DIM * (copy + 1), c % W_SLOTS, :, :].bitcast(f32)
                        .rearrange("a (g t) m -> a g (t m)", g=QUAD),
                        w_parts[copy // 2, c].rearrange("(g a) m -> a g m", g=QUAD),
                    ).then_inc(w_spread[c % W_SLOTS], 16)

            for c in range(W_SLOTS):
                store_parts(c)
            for c in range(W_SLOTS):
                spread(c)
            for c in range(W_SLOTS, W_CHUNKS):
                store_parts(c)
            sp.dma_start(w1_sb[:], w1.rearrange("c p n -> p c n")).then_inc(tail_loaded, 16)
            sp.dma_start(w2_sb[:], w2.rearrange("(m p) n -> p m n", p=LANES)).then_inc(tail_loaded, 16)
            sp.dma_start(w3_sb[:], w3).then_inc(tail_loaded, 16)
            sp.dma_start(b1_sb[:], b1).then_inc(tail_loaded, 16)
            sp.dma_start(b2_sb[:], b2).then_inc(tail_loaded, 16)
            sp.dma_start(dense_sb[:], dense_t).then_inc(tail_loaded, 16)
            sp.dma_start(placing_sb[:], placing).then_inc(tail_loaded, 16)
            for c in range(W_SLOTS, W_CHUNKS):
                spread(c)
            sp.wait_ge(y_kept, 1)
            sp.dma_start(out, y_sb[:]).then_inc(stored, 16)
            sp.wait_ge(stored, 16)

        @block.scalar
        def _(act):
            def cut_w_heads(c):
                act.wait_ge(w_loaded[c % 2], 16 * (c // 2 + 1))
                if c >= 2:
                    act.wait_ge(w_stored[c % 2], 32 * (c // 2))
                act.activation(w_head[:, c % 2, :], w_raw[:, c % 2, :], ACT.Copy).then_inc(w_heads_cut, 1)

            def cut_item_heads(turn):
                pair = turn[1]
                p = ITEM_PAIRS.index(pair)
                if p >= SPLIT_SLOTS:
                    act.wait_ge(turned, TURN_INDEX["items", ITEM_PAIRS[p - SPLIT_SLOTS]] + 1)
                for k, j in enumerate(pair):
                    act.wait_ge(gathered[j], 16 * BATCH_TILES)
                    act.activation(split_sb[:, p % SPLIT_SLOTS, :, k, 0, :], item_rows(j),
                                   ACT.Copy).then_inc(heads_cut, 1)

            def lift(turn):
                kind, k = turn
                act.wait_ge(turned, TURN_INDEX[turn] + 1)
                if kind == "items":
                    for i, j in enumerate(k):
                        for low in (0, 2 * DIM):
                            last = act.activation(stack_sb[low:low + 2 * DIM, j, :],
                                                  turn_ps[2 * DIM * i:2 * DIM * (i + 1), :], ACT.Copy)
                    last.then_inc(lifted, 1)
                elif k < LAST_BLOCK:
                    act.activation(factor_sb[:, k, :], turn_ps[:], ACT.Copy).then_inc(lifted, 1)
                else:
                    act.activation(factor_sb[0:2 * DIM, k, :], turn_ps[0:2 * DIM, :],
                                   ACT.Copy).then_inc(lifted, 1)

            def mix(m):
                lower, upper = (2 * m, 2 * m + 1) if 2 * m + 1 < LAST_BLOCK else (LAST_BLOCK, 2 * m)
                act.wait_ge(lifted, max(TURN_INDEX["block", n] for n in (lower, upper)) + 1)
                if m >= MIXED_SLOTS:
                    act.wait_ge(multiplied, MIXED_UNIT[m - MIXED_SLOTS] + 1)
                for low, n in ((0, lower), (2 * DIM, upper)):
                    last = act.activation(factor_sb[low:low + 2 * DIM, factor_slot(("mixed", m)), :],
                                          factor_sb[low:low + 2 * DIM, n, :], ACT.Copy)
                last.then_inc(mixed_made, 1)

            def keep_z(c):
                act.wait_ge(summed, Z_LAST_ROUND[c] + 1)
                act.activation(z_sb[:, c, :], z_ps[:], ACT.Copy).then_inc(z_kept, 1)

            act.wait_ge(constants_loaded, 32)
            act.activation(identity_r[:], identity_sb[:], ACT.Copy).then_inc(identity_rounded, 1)
            for turn in EARLY_TURNS[0]:
                for c in w_chunks_before(turn):
                    cut_w_heads(c)
                cut_item_heads(turn)
                lift(turn)
            for r in range(ROUNDS):
                if r:
                    for turn in EARLY_TURNS[r]:
                        lift(turn)
                for turn in EARLY_TURNS[r + 1] if r + 1 < ROUNDS else []:
                    for c in w_chunks_before(turn):
                        cut_w_heads(c)
                    cut_item_heads(turn)
                for turn in LATE_TURNS[r]:
                    lift(turn)
                    if turn[1] % 2:
                        mix(mixed_of(turn[1]))
                if r - 1 in Z_LAST_ROUND:
                    keep_z(Z_LAST_ROUND.index(r - 1))
            keep_z(Z_CHUNKS - 1)
            act.wait_ge(tail_loaded, TAIL_LOADS)
            for m in range(M1):
                act.wait_ge(hidden1_made, m + 1)
                act.activation(hidden1_sb[:, m, :], hidden1_ps[m], ACT.Relu,
                               bias=b1_sb[:, m:m + 1]).then_inc(hidden1_kept, 1)
            for m in range(M2):
                act.wait_ge(hidden2_made, m + 1)
                act.activation(hidden2_sb[:, m, :], hidden2_ps[m], ACT.Relu,
                               bias=b2_sb[:, m:m + 1]).then_inc(hidden2_kept, 1)
            act.wait_ge(y_made, 1)
            act.activation(y_sb[:], y_ps, ACT.Copy).then_inc(y_kept, 1)

        @block.vector
        def _(dve):
            dve.memset(factor_sb[2 * DIM:LANES, LAST_BLOCK, :], 0.0).then_inc(last_block_cleared, 1)

            def cut_w_rests(c):
                dve.wait_ge(w_heads_cut, c + 1)
                dve.tensor_tensor(w_rest[:, c % 2, :], w_raw[:, c % 2, :], w_head[:, c % 2, :].bitcast(f32),
                                  ALU.subtract).then_inc(w_rests_cut, 1)

            def cut_item_rests(turn):
                pair = turn[1]
                slot = split_sb[:, ITEM_PAIRS.index(pair) % SPLIT_SLOTS]
                for k, j in enumerate(pair):
                    dve.wait_ge(heads_cut, j + 1)
                    dve.tensor_tensor(slot[:, :, k, 1, :], item_rows(j), slot[:, :, k, 0, :].bitcast(f32),
                                      ALU.subtract).then_inc(rests_cut, 1)

            def multiply(k):
                factors = [TILES[s][0] for s in (2 * k, 2 * k + 1)]
                low, high = (factor_slot(f) for f in factors)
                if low == high:
                    factor = factor_sb[:, low:low + 1, :].broadcast_to([LANES, 2, BATCH])
                else:
                    factor = factor_sb[:, low:high + 1:high - low, :]
                dve.wait_ge(u_made, k + 1)
                for f in factors:
                    if f[0] == "block":
                        dve.wait_ge(lifted, TURN_INDEX[f] + 1)
                    else:
                        dve.wait_ge(mixed_made, f[1] + 1)
                    if f == ("block", LAST_BLOCK):
                        dve.wait_ge(last_block_cleared, 1)
                if k >= PRODUCT_SLOTS:
                    dve.wait_ge(summed, (k - PRODUCT_SLOTS) // 2 + 1)
                half = 2 * (k % 2)
                dve.tensor_tensor(product_sb[:, k % PRODUCT_SLOTS, :, :], u_ps[:, half:half + 2, :],
                                  factor, ALU.mult).then_inc(multiplied, 1)

            for turn in EARLY_TURNS[0]:
                for c in w_chunks_before(turn):
                    cut_w_rests(c)
                cut_item_rests(turn)
            for r in range(ROUNDS):
                multiply(2 * r)
                for turn in EARLY_TURNS[r + 1] if r + 1 < ROUNDS else []:
                    for c in w_chunks_before(turn):
                        cut_w_rests(c)
                    cut_item_rests(turn)
                if 2 * r + 1 < UNITS:
                    multiply(2 * r + 1)

        @block.tensor
        def _(pe):
            def turn(what):
                kind, k = what
                pe.wait_ge(lifted, TURN_INDEX[what])
                if kind == "items":
                    pe.wait_ge(rests_cut, k[-1] + 1)
                    for t in range(BATCH_TILES):
                        source = split_sb[:, ITEM_PAIRS.index(k) % SPLIT_SLOTS, t, 0:len(k)]
                        last = nc.tensor.matmul(turn_ps[0:2 * DIM * len(k), LANES * t:LANES * (t + 1)],
                                                source.rearrange("p i h d -> p (i h d)"), identity_r[:],
                                                start=True, stop=True)
                else:
                    items = QUAD if k < LAST_BLOCK else 2
                    for j in range(QUAD * k, QUAD * k + items):
                        pe.wait_ge(gathered[j], 16 * BATCH_TILES)
                    for t in range(BATCH_TILES):
                        last = nc.tensor.transpose(turn_ps[0:items * DIM, LANES * t:LANES * (t + 1)],
                                                   rows_sb[:, k, t, 0:items, :].rearrange("p q d -> p (q d)"),
                                                   identity_sb[:])
                last.then_inc(turned, 1)

            first_pass = [0]
            for _, passes in TILES:
                first_pass.append(first_pass[-1] + len(passes))

            def contract(k):
                if k >= 2:
                    pe.wait_ge(multiplied, k - 1)
                for s in (2 * k, 2 * k + 1):
                    passes = TILES[s][1]
                    for n, (j, _) in enumerate(passes):
                        c, slot = divmod(first_pass[s] + n, CHUNK_TILES)
                        if slot == 0:
                            pe.wait_ge(w_spread[c % W_SLOTS], 16 * QUAD * (c // W_SLOTS + 1))
                        pe.wait_ge(lifted, ITEM_TURN[j] + 1)
                        last = nc.tensor.matmul(u_ps[:, s % 4, :], w_sb[:, c % W_SLOTS, slot, :],
                                                stack_sb[:, j, :],
                                                start=n == 0, stop=n == len(passes) - 1)
                last.then_inc(u_made, 1)

            def place_dense():
                pe.wait_ge(tail_loaded, TAIL_LOADS)
                pe.wait_ge(z_kept, Z_CHUNKS - 1)
                for half in range(2):
                    group = QUAD - 2 + half
                    nc.tensor.matmul(z_ps[DIM * group:DIM * (group + 1), :], placing_sb[:, half, :], dense_sb[:],
                                     start=True, stop=False, tile_position=(0, DIM * group))

            def add_up(r):
                tiles = range(QUAD * r, min(QUAD * (r + 1), N_TILES))
                pe.wait_ge(multiplied, tiles[-1] // 2 + 1)
                for s in tiles:
                    chunk, group, row = z_place(s)
                    if row == 0 and chunk:
                        pe.wait_ge(z_kept, chunk)
                    dense = chunk == Z_CHUNKS - 1 and group >= QUAD - 2
                    last = nc.tensor.matmul(
                        z_ps[DIM * group:DIM * (group + 1), :],
                        summing_sb[:, DIM - row:2 * DIM - row],
                        product_sb[:, (s // 2) % PRODUCT_SLOTS, s % 2, :],
                        start=row == 0 and not dense, stop=s + QUAD >= N_TILES or z_place(s + QUAD)[0] > chunk,
                        tile_position=(0, DIM * group))
                last.then_inc(summed, 1)

            def layer1(m, c):
                pe.wait_ge(z_kept, c + 1)
                last = nc.tensor.matmul(hidden1_ps[m], w1_sb[:, c, LANES * m:LANES * (m + 1)], z_sb[:, c, :],
                                        start=c == 0, stop=c == Z_CHUNKS - 1)
                if c == Z_CHUNKS - 1:
                    last.then_inc(hidden1_made, 1)

            pe.wait_ge(constants_loaded, 32)
            pe.wait_ge(identity_rounded, 1)
            for r in range(ROUNDS):
                for what in EARLY_TURNS[r]:
                    turn(what)
                contract(2 * r)
                if 2 * r + 1 < UNITS:
                    contract(2 * r + 1)
                if r - 2 == Z_LAST_ROUND[-2]:
                    place_dense()
                if r:
                    add_up(r - 1)
                for what in LATE_TURNS[r]:
                    turn(what)
                if r - 3 in Z_LAST_ROUND:
                    for m in range(2):
                        layer1(m, Z_LAST_ROUND.index(r - 3))
                if r > LAST_TURN_ROUND:
                    pe.wait_ge(lifted, len(TURN_ORDER))
                    done = 2 * (r - LAST_TURN_ROUND - 1)
                    for c in range(min(done, Z_CHUNKS - 1), min(done + 2, Z_CHUNKS - 1)):
                        layer1(2, c)
            pe.wait_ge(multiplied, UNITS - 1)
            layer1(3, 0)
            add_up(ROUNDS - 1)
            for c in range(1, Z_CHUNKS - 1):
                layer1(3, c)
            for m in range(M1):
                layer1(m, Z_CHUNKS - 1)
            for m in range(M1):
                pe.wait_ge(hidden1_kept, m + 1)
                for n in range(M2):
                    last = nc.tensor.matmul(hidden2_ps[n], w2_sb[:, m, LANES * n:LANES * (n + 1)],
                                            hidden1_sb[:, m, :], start=m == 0, stop=m == M1 - 1)
                    if m == M1 - 1:
                        last.then_inc(hidden2_made, 1)
            for n in range(M2):
                pe.wait_ge(hidden2_kept, n + 1)
                last = nc.tensor.matmul(y_ps, w3_sb[:, n:n + 1], hidden2_sb[:, n, :],
                                        start=n == 0, stop=n == M2 - 1)
            last.then_inc(y_made, 1)


def lay_out_w(w):
    flat = np.zeros((DIM, W_CHUNKS * CHUNK_TILES, QUAD, DIM), w.dtype)
    for k, (s, j, pairs) in enumerate(PASSES):
        for q, i in pairs.items():
            flat[:, k, q, :] = w[:, pair_index(i, j), :] if i < j else w[:, pair_index(j, i), :].T
    flat = flat.reshape(DIM, W_CHUNKS, QUAD, STAGED * LANES)
    return np.ascontiguousarray(flat.transpose(1, 2, 0, 3).reshape(W_CHUNKS, LANES, STAGED * LANES))


def lay_out_w1(w1):
    rows = np.zeros((Z_CHUNKS, LANES, HIDDEN1), w1.dtype)
    for s, j, pairs in PASSES:
        chunk, group, row = z_place(s)
        for q, i in pairs.items():
            rows[chunk, DIM * group + row + q] = w1[pair_index(min(i, j), max(i, j))]
    for half in range(2):
        start = DIM * (QUAD - 2 + half) + DENSE_ROW
        rows[-1, start:start + DENSE_HALF] = w1[ITEMS * (ITEMS - 1) // 2 + DENSE_HALF * half:][:DENSE_HALF]
    return rows


def kernel(**inputs):
    import concourse.bacc as bacc
    from concourse.bass_utils import run_bass_kernel_spmd

    given = {k: np.asarray(v) for k, v in inputs.items()}
    summing = np.zeros((LANES, WINDOW), np.float32)
    for q in range(QUAD):
        summing[DIM * q:DIM * (q + 1), DIM + q] = 1.0
    placing = np.zeros((DENSE, 2, DIM), np.float32)
    for k in range(DENSE):
        placing[k, k // DENSE_HALF, DENSE_ROW + k % DENSE_HALF] = 1.0
    arrays = {
        "dense_t": np.ascontiguousarray(given["dense_ctx"].T),
        "ids": given["ids"],
        "w_tiles": lay_out_w(given["L0_rec_w"]),
        "w1": lay_out_w1(given["W_top1"]),
        "b1": np.ascontiguousarray(given["b_top1"].reshape(M1, LANES).T),
        "w2": given["W_top2"],
        "b2": np.ascontiguousarray(given["b_top2"].reshape(M2, LANES).T),
        "w3": np.ascontiguousarray(given["W_top3"].reshape(M2, LANES).T),
        "identity": np.eye(LANES, dtype=np.float32),
        "summing": summing,
        "placing": placing,
    }
    arrays.update({f"tbl_{j}": given[f"tbl_{j}"] for j in range(ITEMS)})

    nc = bacc.Bacc("TRN2", target_bir_lowering=False, num_devices=1)
    aps = {name: nc.dram_tensor(f"in_{name}", a.shape, mybir.dt.from_np(a.dtype), kind="ExternalInput").ap()
           for name, a in arrays.items()}
    out = nc.dram_tensor("out_y", (1, BATCH), mybir.dt.float32, kind="ExternalOutput").ap()
    tables = [aps.pop(f"tbl_{j}") for j in range(ITEMS)]
    build(nc, tables=tables, out=out, **aps)
    run = run_bass_kernel_spmd(nc, [{f"in_{name}": a for name, a in arrays.items()}], core_ids=[0])
    return run.results[0]["out_y"].reshape(BATCH, 1)
```

```python
import numpy as np
from contextlib import ExitStack

import concourse.bass as bass
import concourse.mybir as mybir

BATCH = 512
ITEMS = 39
DIM = 32
DENSE = 16
HIDDEN1 = 512
HIDDEN2 = 256
LANES = 128
QUAD = 4
BATCH_TILES = BATCH // LANES
BLOCKS = -(-ITEMS // QUAD)
LAST_BLOCK = BLOCKS - 1
LAST = ITEMS - 1
CHUNK_TILES = 16
STAGED = CHUNK_TILES // QUAD
WINDOW = 2 * DIM + QUAD
M1 = HIDDEN1 // LANES
M2 = HIDDEN2 // LANES
MIXED_SLOTS = 2


def pair_index(i, j):
    return i * (2 * ITEMS - i - 1) // 2 + j - i - 1


def mixed_of(n):
    return n // 2 if n < LAST_BLOCK else LAST_BLOCK // 2


def plan_tiles():
    lower_inside = [(3, {1: 1, 2: 2}), (0, {3: 3}), (1, {0: 0})]
    lower_mixed = (2, {0: 0, 1: 1})
    upper_inside = [(1, {0: 0, 3: 3}), (2, {1: 1}), (3, {2: 2})]
    upper_mixed = (0, {2: 2, 3: 3})

    def moved(n, one):
        return QUAD * n + one[0], {q: QUAD * n + i for q, i in one[1].items()}

    tiles = []
    for j in range(ITEMS):
        n = j // QUAD
        tiles += [(("block", b), [(j, {q: QUAD * b + q for q in range(QUAD)})]) for b in range(n)]
        if j % QUAD == QUAD - 1:
            upper = n % 2 or n == LAST_BLOCK - 1
            inside = upper_inside if upper else lower_inside
            tiles.append((("block", n), [moved(n, one) for one in inside]))
            if n % 2:
                tiles.append((("mixed", mixed_of(n)), [moved(n - 1, lower_mixed), moved(n, upper_mixed)]))
        elif j == LAST - 1:
            tiles.append((("mixed", mixed_of(n)), [moved(n, (1, {0: 0})), moved(n - 1, upper_mixed)]))
        elif j == LAST:
            tiles.append((("block", n), [moved(n, lower_mixed)]))
    return [t for k in range(0, len(tiles), 2) for t in sorted(tiles[k:k + 2], key=lambda t: factor_slot(t[0]))]


def factor_slot(factor):
    kind, k = factor
    return k if kind == "block" else BLOCKS + k % MIXED_SLOTS


TILES = plan_tiles()
N_TILES = len(TILES)
PASSES = [(s, j, pairs) for s, (factor, passes) in enumerate(TILES) for j, pairs in passes]
UNITS = N_TILES // 2
ROUNDS = -(-N_TILES // QUAD)
W_CHUNKS = -(-len(PASSES) // CHUNK_TILES)
W_SLOTS = 2
CHUNK_ROUNDS = DIM // QUAD
Z_CHUNKS = -(-ROUNDS // CHUNK_ROUNDS)
Z_LAST_ROUND = [min(CHUNK_ROUNDS * (c + 1), ROUNDS) - 1 for c in range(Z_CHUNKS)]
DENSE_HALF = DENSE // 2
DENSE_ROW = DIM - DENSE_HALF
assert N_TILES % QUAD == 2 and QUAD * (ROUNDS - 1) <= DIM * (Z_CHUNKS - 1) + DENSE_ROW
PRODUCT_SLOTS = 4
SPLIT_SLOTS = 3
LOOKED_UP = 2 * QUAD
SHORT_ROWS = 1000
TABLE_CHUNKS = 8
CHUNK_ROWS = SHORT_ROWS // TABLE_CHUNKS
HALVES = 2
HALF_CHUNKS = TABLE_CHUNKS // HALVES
ONE_HOT_SLOTS = 4
LAST_LOOKED_UP = (LOOKED_UP - 2, LOOKED_UP - 1)
GATHERED_BLOCK = LOOKED_UP // QUAD
assert CHUNK_ROWS <= LANES and CHUNK_ROWS * TABLE_CHUNKS == SHORT_ROWS
assert {tuple(sorted((i, j))) for s, j, pairs in PASSES for i in pairs.values()} == {
    (i, j) for j in range(ITEMS) for i in range(j)}


def units_before(c):
    return PASSES[min(CHUNK_TILES * (c + 1), len(PASSES)) - 1][0] // 2 + 1


def z_place(s):
    r = s // QUAD
    return r // CHUNK_ROUNDS, s % QUAD, QUAD * (r % CHUNK_ROUNDS)


def first_round(wanted):
    return min(s for s, t in enumerate(TILES) if wanted(t)) // QUAD


LAST_MADE = ("block", GATHERED_BLOCK - 1)
ONE_AHEAD_ROUNDS = 8


def plan_turns():
    pairs = [(j, j + 1) for j in range(0, LAST - 2, 2)] + [(LAST - 2,), (LAST - 1,), (LAST,)]
    uses = []
    for pair in pairs:
        uses.append((first_round(lambda t: any(j in pair for j, _ in t[1])), ("items", pair)))
    for n in range(GATHERED_BLOCK, BLOCKS):
        uses.append((first_round(lambda t: t[0] == ("block", n) or t[0] == ("mixed", mixed_of(n)) and n * QUAD in
                                 [i - i % QUAD for _, p in t[1] for i in p.values()]), ("block", n)))
    ahead, turns, free = [], [None] * ROUNDS, ROUNDS - 1
    for use, turn in sorted(uses, reverse=True):
        r = min(use - (1 if use < ONE_AHEAD_ROUNDS else 2), free)
        if r > 0:
            turns[r], free = turn, r - 1
        else:
            ahead.insert(0, turn)
    place = ahead.index(("items", LAST_LOOKED_UP))
    ahead[place:place] = [("block", n) for n in range(GATHERED_BLOCK - 1)]
    ahead.append(LAST_MADE)
    return ahead, turns


TURNS_AHEAD, TURNS = plan_turns()
assert TURNS[1][0] == "items"
FIRST_PAIRS = sum(kind == "items" for kind, _ in TURNS_AHEAD)
TURN_ORDER = TURNS_AHEAD + [t for t in TURNS if t]
TURN_INDEX = {t: k for k, t in enumerate(TURN_ORDER)}
ITEM_TURN = {j: TURN_INDEX[t] for t in TURN_ORDER if t[0] == "items" for j in t[1]}
ITEM_PAIRS = [t[1] for t in TURN_ORDER if t[0] == "items"]
LAST_TURN_ROUND = max(r for r in range(ROUNDS) if TURNS[r])
IN_TURNING_BANK = [t for t in TURN_ORDER
                   if t != LAST_MADE and (t[0] == "block" or t[1][0] >= LOOKED_UP)]
GATHERED_PAIRS = [pair for pair in ITEM_PAIRS if pair[0] >= LOOKED_UP]
MIXED_UNIT = {t[0][1]: s // 2 for s, t in enumerate(TILES) if t[0][0] == "mixed"}

EARLY_CHUNKS = 2


def first_chunk(m):
    return EARLY_CHUNKS if m >= 2 else 0


def plan_fillers():
    def halves(m, c):
        return [(m, c, None)] if c in (0, first_chunk(m)) else [(m, c, half) for half in range(2)]

    fillers, queue = [None] * ROUNDS, []
    resume = 0
    waiting = [part for c in range(EARLY_CHUNKS, Z_CHUNKS - 1) for part in halves(2, c)]
    for r in range(ROUNDS):
        if r - 2 in Z_LAST_ROUND[:-1]:
            c = Z_LAST_ROUND.index(r - 2)
            queue += [part for m in ((2, 3) if c < EARLY_CHUNKS else (0, 1)) for part in halves(m, c)]
            if c == EARLY_CHUNKS - 1:
                queue += [part for done in range(EARLY_CHUNKS) for m in (0, 1) for part in halves(m, done)]
        if r > LAST_TURN_ROUND and not queue and r - 2 >= Z_LAST_ROUND[waiting[0][1]]:
            queue.append(waiting.pop(0))
        if queue and r >= resume and (not TURNS[r] or TURNS[r][0] == "items"):
            fillers[r] = queue.pop(0)
            if fillers[r] == (3, EARLY_CHUNKS - 1, 1):
                resume = r + 3
    return fillers, queue + waiting


FILLERS, UNFILLED = plan_fillers()
EARLY_ROUND = FILLERS.index((3, EARLY_CHUNKS - 1, 1))
W_CUT_HALVES = [4, 7, 12, 15]
W_HEADS_AHEAD = {0: (0, 1), 2: (2, 3)}
W_CUT_AHEAD = len(W_CUT_HALVES)
W_CUT_ROUND = {2 * (c - W_CUT_AHEAD) + 1: c for c in range(W_CUT_AHEAD, W_CHUNKS)}


def one_hot_index(pair, half, j):
    return HALVES * pair[0] + 2 * half + j - pair[0]


def build(nc, order, dense_t, ids, short_ids, short_tables, table_rows, tables, w_tiles, w1, b1, w2, b2, w3,
          identity, summing, placing, selecting, out):
    f32 = mybir.dt.float32
    f32r = mybir.dt.float32r
    ALU = mybir.AluOpType
    ACT = mybir.ActivationFunctionType

    with ExitStack() as stack:
        def sbuf(name, shape, dtype=f32):
            return stack.enter_context(nc.sbuf_tensor(name, shape, dtype))

        def psum(name, shape):
            return stack.enter_context(nc.psum_tensor(name, shape, f32))

        def sem(name):
            return stack.enter_context(nc.semaphore(name))

        ids_sb = sbuf("ids_sb", [LANES, BATCH_TILES, ITEMS], mybir.dt.int32)
        identity_sb = sbuf("identity_sb", [LANES, LANES])
        identity_r = sbuf("identity_r", [LANES, LANES], f32r)
        summing_sb = sbuf("summing_sb", [LANES, WINDOW])
        placing_sb = sbuf("placing_sb", [DENSE, 2, DIM])
        dense_sb = sbuf("dense_sb", [DENSE, BATCH])
        selecting_sb = sbuf("selecting_sb", [2 * DIM, (2 * QUAD - 1) * DIM])
        selecting_r = sbuf("selecting_r", [2 * DIM, (2 * QUAD - 1) * DIM], f32r)
        table_rows_sb = sbuf("table_rows_sb", [CHUNK_ROWS, TABLE_CHUNKS])
        rows_sb = sbuf("rows_sb", [LANES, BLOCKS - GATHERED_BLOCK, BATCH_TILES, QUAD, DIM])
        split_sb = sbuf("split_sb", [LANES, SPLIT_SLOTS, BATCH_TILES, 2, 2, DIM], f32r)
        stack_sb = sbuf("stack_sb", [LANES, ITEMS, BATCH], f32r)
        factor_sb = sbuf("factor_sb", [LANES, BLOCKS + MIXED_SLOTS, BATCH])
        w_raw = sbuf("w_raw", [LANES, 2, STAGED * LANES])
        w_head = sbuf("w_head", [LANES, 2, STAGED * LANES], f32r)
        w_rest = sbuf("w_rest", [LANES, 2, STAGED * LANES], f32r)
        w_parts = nc.dram_tensor("w_parts", (2, W_CHUNKS, LANES, STAGED * LANES), f32).ap()
        w_sb = sbuf("w_sb", [LANES, W_SLOTS, CHUNK_TILES, LANES], f32r)
        product_sb = sbuf("product_sb", [LANES, PRODUCT_SLOTS, 2, BATCH])
        z_w1_sb = sbuf("z_w1_sb", [LANES, 2 * Z_CHUNKS, BATCH])
        z_sb = z_w1_sb[:, 0:Z_CHUNKS, :]
        w1_sb = z_w1_sb[:, Z_CHUNKS:2 * Z_CHUNKS, :]
        short_ids_sb = z_w1_sb[0:CHUNK_ROWS, 0:LOOKED_UP, :].bitcast(mybir.dt.int32)
        short_raw = z_w1_sb[0:CHUNK_ROWS, LOOKED_UP:LOOKED_UP + LOOKED_UP // 2, :].rearrange(
            "p s (k c d) -> p (s k) c d", k=2, c=TABLE_CHUNKS)
        short_split = stack_sb[0:CHUNK_ROWS, ITEMS - LOOKED_UP:ITEMS, :].rearrange(
            "p s (c k) -> p s c k", c=TABLE_CHUNKS)
        one_hot_at = ITEMS - LOOKED_UP - ONE_HOT_SLOTS * HALF_CHUNKS
        one_hot_sb = stack_sb[0:CHUNK_ROWS, one_hot_at:ITEMS - LOOKED_UP, :].rearrange(
            "p (s c) b -> p s c b", s=ONE_HOT_SLOTS)
        w2_sb = sbuf("w2_sb", [LANES, M1, HIDDEN2])
        w3_sb = sbuf("w3_sb", [LANES, M2])
        b1_sb = sbuf("b1_sb", [LANES, M1])
        b2_sb = sbuf("b2_sb", [LANES, M2])
        early_sb = sbuf("early_sb", [LANES, 2, BATCH])
        rows_flat = rows_sb[:].rearrange("p n t q d -> p (n t q d)")
        hidden1_sb = rows_flat[:, 0:M1 * BATCH].rearrange("p (m b) -> p m b", m=M1)
        hidden2_sb = rows_flat[:, M1 * BATCH:(M1 + M2) * BATCH].rearrange("p (m b) -> p m b", m=M2)
        y_sb = rows_flat[0:1, (M1 + M2) * BATCH:(M1 + M2 + 1) * BATCH]

        u_ps = psum("u_ps", [LANES, 4, BATCH])
        z_ps = psum("z_ps", [LANES, BATCH])
        turn_ps = psum("turn_ps", [LANES, BATCH])
        hidden_ps = psum("hidden_ps", [LANES, 2, BATCH])
        ending = 2 * ((UNITS - 1) % 2)
        free = 2 - ending
        hidden1_ps = [hidden_ps[:, 0, :], hidden_ps[:, 1, :], turn_ps[:], u_ps[:, free, :]]
        hidden2_ps = [u_ps[:, free + 1, :], u_ps[:, ending, :]]
        y_ps = u_ps[0:1, ending + 1, :]

        ids_loaded = sem("ids_loaded")
        constants_loaded = sem("constants_loaded")
        CONSTANT_LOADS = 3 * 16
        constants_rounded = sem("constants_rounded")
        table_rows_loaded = sem("table_rows_loaded")
        short_tables_loaded = [sem(f"short_tables_loaded_{p}") for p in range(2)]
        short_ids_loaded = [sem(f"short_ids_loaded_{p}") for p in range(LOOKED_UP // 2)]
        one_hots_made = sem("one_hots_made")
        one_hots_used = sem("one_hots_used")
        w1_loaded = sem("w1_loaded")
        tail_loaded = sem("tail_loaded")
        gathered = {j: sem(f"gathered_{j}") for j in range(LOOKED_UP, ITEMS)}
        heads_cut = sem("heads_cut")
        rests_cut = sem("rests_cut")
        turned = sem("turned")
        lifted = sem("lifted")
        mixed_made = sem("mixed_made")
        w_loaded = [sem(f"w_loaded_{s}") for s in range(2)]
        w_heads_cut = sem("w_heads_cut")
        w_rests_cut = sem("w_rests_cut")
        w_stored = [sem(f"w_stored_{s}") for s in range(2)]
        w_spread = [sem(f"w_spread_{s}") for s in range(W_SLOTS)]
        u_made = sem("u_made")
        multiplied = sem("multiplied")
        summed = sem("summed")
        z_kept = sem("z_kept")
        last_block_cleared = sem("last_block_cleared")
        early_made = sem("early_made")
        early_kept = sem("early_kept")
        hidden1_made = sem("hidden1_made")
        hidden1_summed = sem("hidden1_summed")
        hidden1_kept = sem("hidden1_kept")
        hidden2_made = sem("hidden2_made")
        hidden2_kept = sem("hidden2_kept")
        y_made = sem("y_made")
        y_kept = sem("y_kept")
        stored = sem("stored")
        TAIL_LOADS = 6 * 16

        block = stack.enter_context(nc.Block())

        def pair_rows(pair):
            q = pair[0] % QUAD
            return rows_sb[:, pair[0] // QUAD - GATHERED_BLOCK, :, q:q + len(pair), :]

        def looked_up(pair):
            return pair[0] < LOOKED_UP

        def block_ps(n):
            return hidden_ps[:, 0, :] if ("block", n) == LAST_MADE else turn_ps[:]

        def look_up_ps(j):
            return u_ps[0:2 * DIM, j % 4, :]

        def split_slot(pair):
            return split_sb[:, GATHERED_PAIRS.index(pair) % SPLIT_SLOTS, :, 0:len(pair)]

        @block.gpsimd
        def _(pool):
            pool.wait_ge(ids_loaded, 16)
            for j in range(LOOKED_UP, ITEMS):
                for t in range(BATCH_TILES):
                    pool.indirect_dma_start(
                        rows_sb[:, j // QUAD - GATHERED_BLOCK, t, j % QUAD, :], None, tables[j],
                        bass.IndirectOffsetOnAxis(ap=ids_sb[:, t, order[j]:order[j] + 1], axis=0),
                    ).then_inc(gathered[j], 16)

        @block.sync
        def _(sp):
            def load_short_ids(p):
                sp.dma_start(short_ids_sb[:, 2 * p:2 * p + 2, :],
                             short_ids[2 * p:2 * p + 2, :].partition_broadcast(CHUNK_ROWS)
                             ).then_inc(short_ids_loaded[p], 16)

            def load_short_tables(k, first, end):
                sp.dma_start(short_raw[:, first:end],
                             short_tables[first:end].rearrange("s (p c) d -> p s c d", c=TABLE_CHUNKS)
                             ).then_inc(short_tables_loaded[k], 16)

            sp.dma_start(ids_sb[:], ids.rearrange("(t p) f -> p t f", p=LANES)).then_inc(ids_loaded, 16)
            load_short_ids(0)
            sp.dma_start(table_rows_sb[:], table_rows).then_inc(table_rows_loaded, 16)
            load_short_tables(0, 0, 2)
            for c in range(2):
                sp.dma_start(w_raw[:, c, :], w_tiles[c]).then_inc(w_loaded[c], 16)
            load_short_ids(1)
            load_short_tables(1, 2, LOOKED_UP)
            sp.dma_start(identity_sb[:], identity).then_inc(constants_loaded, 16)
            sp.dma_start(selecting_sb[:], selecting).then_inc(constants_loaded, 16)
            sp.dma_start(summing_sb[:], summing).then_inc(constants_loaded, 16)
            for p in range(2, LOOKED_UP // 2):
                load_short_ids(p)

            def store_parts(c):
                sp.wait_ge(w_heads_cut, c + 1)
                sp.dma_start(w_parts[0, c], w_head[:, c % 2, :].bitcast(f32)).then_inc(w_stored[c % 2], 16)
                sp.wait_ge(w_rests_cut, c + 1)
                sp.dma_start(w_parts[1, c], w_rest[:, c % 2, :].bitcast(f32)).then_inc(w_stored[c % 2], 16)
                if c + 2 < W_CHUNKS:
                    sp.dma_start(w_raw[:, c % 2, :], w_tiles[c + 2]).then_inc(w_loaded[c % 2], 16)

            def spread(c):
                sp.wait_ge(w_stored[c % 2], 32 * (c // 2 + 1))
                if c >= W_SLOTS:
                    sp.wait_ge(u_made, units_before(c - W_SLOTS))
                for copy in range(QUAD):
                    sp.dma_start(
                        w_sb[DIM * copy:DIM * (copy + 1), c % W_SLOTS, :, :].bitcast(f32)
                        .rearrange("a (g t) m -> a g (t m)", g=QUAD),
                        w_parts[copy // 2, c].rearrange("(g a) m -> a g m", g=QUAD),
                    ).then_inc(w_spread[c % W_SLOTS], 16)

            for c in range(W_SLOTS):
                store_parts(c)
                spread(c)
            for c in range(W_SLOTS, W_CUT_AHEAD):
                store_parts(c)
            sp.dma_start(w2_sb[:], w2.rearrange("(m p) n -> p m n", p=LANES)).then_inc(tail_loaded, 16)
            sp.dma_start(w3_sb[:], w3).then_inc(tail_loaded, 16)
            sp.dma_start(b1_sb[:], b1).then_inc(tail_loaded, 16)
            sp.dma_start(b2_sb[:], b2).then_inc(tail_loaded, 16)
            sp.dma_start(dense_sb[:], dense_t).then_inc(tail_loaded, 16)
            sp.dma_start(placing_sb[:], placing).then_inc(tail_loaded, 16)
            sp.wait_ge(one_hots_made, LOOKED_UP * HALVES)
            sp.dma_start(w1_sb, w1.rearrange("c p n -> p c n")).then_inc(w1_loaded, 16)
            spread_round = {c: (units_before(c - W_SLOTS) - 1) // 2 for c in range(W_SLOTS, W_CHUNKS)}
            for r in range(ROUNDS):
                if r in W_CUT_ROUND:
                    store_parts(W_CUT_ROUND[r])
                for c in range(W_SLOTS, W_CHUNKS):
                    if spread_round[c] == r:
                        spread(c)
            sp.wait_ge(y_kept, 1)
            sp.dma_start(out, y_sb).then_inc(stored, 16)
            sp.wait_ge(stored, 16)

        @block.scalar
        def _(act):
            def cut_w_heads(c):
                act.wait_ge(w_loaded[c % 2], 16 * (c // 2 + 1))
                if c >= 2:
                    act.wait_ge(w_stored[c % 2], 32 * (c // 2))
                act.activation(w_head[:, c % 2, :], w_raw[:, c % 2, :], ACT.Copy).then_inc(w_heads_cut, 1)

            def cut_item_heads(turn):
                pair = turn[1]
                if looked_up(pair):
                    act.wait_ge(short_tables_loaded[min(pair[0], 1)], 16)
                    act.activation(short_split[:, pair[0]:pair[-1] + 1, :, 0:DIM],
                                   short_raw[:, pair[0]:pair[-1] + 1], ACT.Copy).then_inc(heads_cut, 1)
                    return
                g = GATHERED_PAIRS.index(pair)
                if g >= SPLIT_SLOTS:
                    act.wait_ge(turned, TURN_INDEX["items", GATHERED_PAIRS[g - SPLIT_SLOTS]] + 1)
                for j in pair:
                    act.wait_ge(gathered[j], 16 * BATCH_TILES)
                act.activation(split_slot(pair)[:, :, :, 0, :], pair_rows(pair), ACT.Copy).then_inc(heads_cut, 1)

            def lift(turn):
                kind, k = turn
                act.wait_ge(turned, TURN_INDEX[turn] + 1)
                if kind == "items" and looked_up(k):
                    for j in k:
                        for low in (0, 2 * DIM):
                            last = act.activation(stack_sb[low:low + 2 * DIM, j, :], look_up_ps(j), ACT.Copy)
                    last.then_inc(lifted, 1)
                elif kind == "items":
                    for i, j in enumerate(k):
                        for low in (0, 2 * DIM):
                            last = act.activation(stack_sb[low:low + 2 * DIM, j, :],
                                                  turn_ps[2 * DIM * i:2 * DIM * (i + 1), :], ACT.Copy)
                    last.then_inc(lifted, 1)
                elif k < LAST_BLOCK:
                    act.activation(factor_sb[:, k, :], block_ps(k), ACT.Copy).then_inc(lifted, 1)
                else:
                    act.activation(factor_sb[0:2 * DIM, k, :], turn_ps[0:2 * DIM, :],
                                   ACT.Copy).then_inc(lifted, 1)

            def mix(m):
                lower, upper = (2 * m, 2 * m + 1) if 2 * m + 1 < LAST_BLOCK else (LAST_BLOCK, 2 * m)
                act.wait_ge(lifted, max(TURN_INDEX["block", n] for n in (lower, upper)) + 1)
                if m >= MIXED_SLOTS:
                    act.wait_ge(multiplied, MIXED_UNIT[m - MIXED_SLOTS] + 1)
                for low, n in ((0, lower), (2 * DIM, upper)):
                    last = act.activation(factor_sb[low:low + 2 * DIM, factor_slot(("mixed", m)), :],
                                          factor_sb[low:low + 2 * DIM, n, :], ACT.Copy)
                last.then_inc(mixed_made, 1)

            def keep_z(c):
                act.wait_ge(summed, Z_LAST_ROUND[c] + 1)
                act.activation(z_sb[:, c, :], z_ps[:], ACT.Copy).then_inc(z_kept, 1)

            def lift_and_mix(turn):
                lift(turn)
                if turn[0] == "block" and turn[1] % 2:
                    mix(mixed_of(turn[1]))

            for pair in ITEM_PAIRS[:2]:
                cut_item_heads(("items", pair))
            for turn in TURNS_AHEAD:
                if turn[0] == "items":
                    p = ITEM_PAIRS.index(turn[1])
                    for c in W_HEADS_AHEAD.get(p, ()):
                        cut_w_heads(c)
                    if p == 0:
                        act.wait_ge(constants_loaded, CONSTANT_LOADS)
                        act.activation(identity_r[:], identity_sb[:], ACT.Copy).then_inc(constants_rounded, 1)
                        act.activation(selecting_r[:], selecting_sb[:], ACT.Copy).then_inc(constants_rounded, 1)
                    if p + 2 <= FIRST_PAIRS:
                        cut_item_heads(("items", ITEM_PAIRS[p + 2]))
                lift_and_mix(turn)
            for r in range(ROUNDS):
                if r + 1 in W_CUT_ROUND:
                    cut_w_heads(W_CUT_ROUND[r + 1])
                if 0 < r < ROUNDS - 1 and TURNS[r + 1] and TURNS[r + 1][0] == "items":
                    cut_item_heads(TURNS[r + 1])
                if TURNS[r]:
                    lift_and_mix(TURNS[r])
                if r - 1 in Z_LAST_ROUND:
                    keep_z(Z_LAST_ROUND.index(r - 1))
                if r - 1 == EARLY_ROUND:
                    act.wait_ge(early_made, 2)
                    act.activation(early_sb[:], hidden_ps[:], ACT.Copy).then_inc(early_kept, 1)
            keep_z(Z_CHUNKS - 1)
            act.wait_ge(tail_loaded, TAIL_LOADS)
            for m in range(M1):
                if m < 2:
                    act.wait_ge(hidden1_made, m + 1)
                    source = hidden1_ps[m]
                else:
                    act.wait_ge(hidden1_summed, m - 1)
                    source = hidden1_sb[:, m, :]
                act.activation(hidden1_sb[:, m, :], source, ACT.Relu,
                               bias=b1_sb[:, m:m + 1]).then_inc(hidden1_kept, 1)
            for m in range(M2):
                act.wait_ge(hidden2_made, m + 1)
                act.activation(hidden2_sb[:, m, :], hidden2_ps[m], ACT.Relu,
                               bias=b2_sb[:, m:m + 1]).then_inc(hidden2_kept, 1)
            act.wait_ge(y_made, 1)
            act.activation(y_sb, y_ps, ACT.Copy).then_inc(y_kept, 1)

        @block.vector
        def _(dve):
            dve.memset(factor_sb[2 * DIM:LANES, LAST_BLOCK, :], 0.0).then_inc(last_block_cleared, 1)

            def cut_w_rests(c):
                dve.wait_ge(w_heads_cut, c + 1)
                dve.tensor_tensor(w_rest[:, c % 2, :], w_raw[:, c % 2, :], w_head[:, c % 2, :].bitcast(f32),
                                  ALU.subtract).then_inc(w_rests_cut, 1)

            def cut_item_rests(turn):
                pair = turn[1]
                dve.wait_ge(heads_cut, ITEM_PAIRS.index(pair) + 1)
                if looked_up(pair):
                    part = short_split[:, pair[0]:pair[-1] + 1]
                    dve.tensor_tensor(part[:, :, :, DIM:2 * DIM], short_raw[:, pair[0]:pair[-1] + 1],
                                      part[:, :, :, 0:DIM].bitcast(f32), ALU.subtract).then_inc(rests_cut, 1)
                    return
                slot = split_slot(pair)
                dve.tensor_tensor(slot[:, :, :, 1, :], pair_rows(pair), slot[:, :, :, 0, :].bitcast(f32),
                                  ALU.subtract).then_inc(rests_cut, 1)

            def multiply(k):
                factors = [TILES[s][0] for s in (2 * k, 2 * k + 1)]
                low, high = (factor_slot(f) for f in factors)
                if low == high:
                    factor = factor_sb[:, low:low + 1, :].broadcast_to([LANES, 2, BATCH])
                else:
                    factor = factor_sb[:, low:high + 1:high - low, :]
                dve.wait_ge(u_made, k + 1)
                for f in factors:
                    if f[0] == "block":
                        dve.wait_ge(lifted, TURN_INDEX[f] + 1)
                    else:
                        dve.wait_ge(mixed_made, f[1] + 1)
                    if f == ("block", LAST_BLOCK):
                        dve.wait_ge(last_block_cleared, 1)
                if k >= PRODUCT_SLOTS:
                    dve.wait_ge(summed, (k - PRODUCT_SLOTS) // 2 + 1)
                half = 2 * (k % 2)
                dve.tensor_tensor(product_sb[:, k % PRODUCT_SLOTS, :, :], u_ps[:, half:half + 2, :],
                                  factor, ALU.mult).then_inc(multiplied, 1)

            def make_one_hots(j, half, n):
                before = n - ONE_HOT_SLOTS
                p, place = divmod(before, 2 * HALVES)
                if before >= 0 and place < 2 * HALVES - 1:
                    dve.wait_ge(one_hots_used, (2 * HALVES - 1) * p + place + 1)
                elif before >= 0:
                    dve.wait_ge(turned, TURN_INDEX["items", (2 * p, 2 * p + 1)] + 1)
                for k in range(HALF_CHUNKS):
                    c = HALF_CHUNKS * half + k
                    last = dve.tensor_scalar(one_hot_sb[:, n % ONE_HOT_SLOTS, k, :], short_ids_sb[:, j, :],
                                             table_rows_sb[:, c:c + 1], None, ALU.is_equal)
                last.then_inc(one_hots_made, 1)

            dve.wait_ge(table_rows_loaded, 16)
            for pair in ITEM_PAIRS[:FIRST_PAIRS]:
                if not looked_up(pair):
                    cut_item_rests(("items", pair))
                    continue
                dve.wait_ge(short_ids_loaded[pair[0] // 2], 16)
                for half in range(HALVES):
                    for j in pair:
                        n = one_hot_index(pair, half, j)
                        make_one_hots(j, half, n)
                        if n % (2 * HALVES) == 0:
                            cut_item_rests(("items", pair))
                        if n in W_CUT_HALVES:
                            cut_w_rests(W_CUT_HALVES.index(n))
            for r in range(ROUNDS):
                multiply(2 * r)
                if r + 1 < ROUNDS and TURNS[r + 1] and TURNS[r + 1][0] == "items":
                    cut_item_rests(TURNS[r + 1])
                if r in W_CUT_ROUND:
                    cut_w_rests(W_CUT_ROUND[r])
                if 2 * r + 1 < UNITS:
                    multiply(2 * r + 1)
            dve.wait_ge(early_kept, 1)
            for m in (2, 3):
                dve.wait_ge(hidden1_made, m + 1)
                dve.tensor_tensor(hidden1_sb[:, m, :], hidden1_ps[m], early_sb[:, m - 2, :],
                                  ALU.add).then_inc(hidden1_summed, 1)

        @block.tensor
        def _(pe):
            def turn(what):
                kind, k = what
                look_up = kind == "items" and looked_up(k)
                if look_up and k[0] >= 4:
                    pe.wait_ge(lifted, TURN_INDEX["items", (k[0] - 4, k[1] - 4)] + 1)
                elif what in IN_TURNING_BANK[1:]:
                    pe.wait_ge(lifted, TURN_INDEX[IN_TURNING_BANK[IN_TURNING_BANK.index(what) - 1]] + 1)
                if look_up:
                    pe.wait_ge(rests_cut, ITEM_PAIRS.index(k) + 1)
                    for half in range(HALVES):
                        if k == LAST_LOOKED_UP and half:
                            pe.wait_ge(lifted, TURN_INDEX["items", (LOOKED_UP - 4, LOOKED_UP - 3)] + 1)
                            contract(0)
                        for i, j in enumerate(k):
                            n = one_hot_index(k, half, j)
                            pe.wait_ge(one_hots_made, n + 1)
                            for m in range(HALF_CHUNKS):
                                c = HALF_CHUNKS * half + m
                                last = nc.tensor.matmul(
                                    look_up_ps(j),
                                    short_split[:, j, c, :],
                                    one_hot_sb[:, n % ONE_HOT_SLOTS, m, :],
                                    start=c == 0, stop=c == TABLE_CHUNKS - 1)
                            if (half, i) != (HALVES - 1, 1):
                                last.then_inc(one_hots_used, 1)
                elif kind == "items":
                    pe.wait_ge(rests_cut, ITEM_PAIRS.index(k) + 1)
                    for t in range(BATCH_TILES):
                        source = split_slot(k)[:, t]
                        last = nc.tensor.matmul(turn_ps[0:2 * DIM * len(k), LANES * t:LANES * (t + 1)],
                                                source.rearrange("p i h d -> p (i h d)"), identity_r[:],
                                                start=True, stop=True)
                elif k < GATHERED_BLOCK:
                    if k == 0:
                        pe.wait_ge(constants_loaded, CONSTANT_LOADS)
                        pe.wait_ge(constants_rounded, 2)
                    pe.wait_ge(lifted, max(ITEM_TURN[j] for j in range(QUAD * k, QUAD * (k + 1))) + 1)
                    for q in range(QUAD):
                        window = DIM * (QUAD - 1 - q)
                        last = nc.tensor.matmul(block_ps(k), selecting_r[:, window:window + LANES],
                                                stack_sb[0:2 * DIM, QUAD * k + q, :],
                                                start=q == 0, stop=q == QUAD - 1)
                else:
                    items = QUAD if k < LAST_BLOCK else 2
                    for j in range(QUAD * k, QUAD * k + items):
                        pe.wait_ge(gathered[j], 16 * BATCH_TILES)
                    for t in range(BATCH_TILES):
                        source = rows_sb[:, k - GATHERED_BLOCK, t, 0:items, :]
                        last = nc.tensor.transpose(turn_ps[0:items * DIM, LANES * t:LANES * (t + 1)],
                                                   source.rearrange("p q d -> p (q d)"), identity_sb[:])
                last.then_inc(turned, 1)

            first_pass = [0]
            for _, passes in TILES:
                first_pass.append(first_pass[-1] + len(passes))

            def contract(k):
                if k >= 2:
                    pe.wait_ge(multiplied, k - 1)
                for s in (2 * k, 2 * k + 1):
                    passes = TILES[s][1]
                    for n, (j, _) in enumerate(passes):
                        c, slot = divmod(first_pass[s] + n, CHUNK_TILES)
                        if slot == 0:
                            pe.wait_ge(w_spread[c % W_SLOTS], 16 * QUAD * (c // W_SLOTS + 1))
                        pe.wait_ge(lifted, ITEM_TURN[j] + 1)
                        last = nc.tensor.matmul(u_ps[:, s % 4, :], w_sb[:, c % W_SLOTS, slot, :],
                                                stack_sb[:, j, :],
                                                start=n == 0, stop=n == len(passes) - 1)
                last.then_inc(u_made, 1)

            def place_dense():
                pe.wait_ge(tail_loaded, TAIL_LOADS)
                pe.wait_ge(z_kept, Z_CHUNKS - 1)
                for half in range(2):
                    group = QUAD - 2 + half
                    nc.tensor.matmul(z_ps[DIM * group:DIM * (group + 1), :], placing_sb[:, half, :], dense_sb[:],
                                     start=True, stop=False, tile_position=(0, DIM * group))

            def add_up(r):
                tiles = range(QUAD * r, min(QUAD * (r + 1), N_TILES))
                pe.wait_ge(multiplied, tiles[-1] // 2 + 1)
                for s in tiles:
                    chunk, group, row = z_place(s)
                    if row == 0 and chunk:
                        pe.wait_ge(z_kept, chunk)
                    dense = chunk == Z_CHUNKS - 1 and group >= QUAD - 2
                    last = nc.tensor.matmul(
                        z_ps[DIM * group:DIM * (group + 1), :],
                        summing_sb[:, DIM - row:2 * DIM - row],
                        product_sb[:, (s // 2) % PRODUCT_SLOTS, s % 2, :],
                        start=row == 0 and not dense, stop=s + QUAD >= N_TILES or z_place(s + QUAD)[0] > chunk,
                        tile_position=(0, DIM * group))
                last.then_inc(summed, 1)

            def layer1(m, c, half=None):
                batch = slice(0, BATCH) if half is None else slice(BATCH // 2 * half, BATCH // 2 * (half + 1))
                pe.wait_ge(w1_loaded, 16)
                pe.wait_ge(z_kept, c + 1)
                early = m >= 2 and c < EARLY_CHUNKS
                if m == 2 and not early:
                    pe.wait_ge(lifted, len(TURN_ORDER))
                if m < 2:
                    pe.wait_ge(early_kept, 1)
                bank = hidden_ps[:, m - 2, :] if early else hidden1_ps[m]
                stop = c == Z_CHUNKS - 1 or early and c == EARLY_CHUNKS - 1 and half == 1
                last = nc.tensor.matmul(bank[:, batch], w1_sb[:, c, LANES * m:LANES * (m + 1)], z_sb[:, c, batch],
                                        start=c == (0 if early else first_chunk(m)), stop=stop)
                if stop:
                    last.then_inc(early_made if early else hidden1_made, 1)

            for what in TURNS_AHEAD:
                if what == LAST_MADE:
                    pe.wait_ge(lifted, TURN_INDEX["items", LAST_LOOKED_UP] + 1)
                    contract(1)
                turn(what)
            for r in range(ROUNDS):
                if r:
                    contract(2 * r)
                if TURNS[r]:
                    turn(TURNS[r])
                if FILLERS[r]:
                    layer1(*FILLERS[r])
                if 0 < r < UNITS // 2:
                    contract(2 * r + 1)
                if r - 2 == Z_LAST_ROUND[-2]:
                    place_dense()
                if r:
                    add_up(r - 1)
            pe.wait_ge(multiplied, UNITS - 1)
            layer1(3, EARLY_CHUNKS)
            add_up(ROUNDS - 1)
            for m, c, half in UNFILLED:
                layer1(m, c, half)
            for c in range(EARLY_CHUNKS + 1, Z_CHUNKS - 1):
                layer1(3, c)
            for m in range(M1):
                layer1(m, Z_CHUNKS - 1)
            for m in range(M1):
                pe.wait_ge(hidden1_kept, m + 1)
                for n in range(M2):
                    last = nc.tensor.matmul(hidden2_ps[n], w2_sb[:, m, LANES * n:LANES * (n + 1)],
                                            hidden1_sb[:, m, :], start=m == 0, stop=m == M1 - 1)
                    if m == M1 - 1:
                        last.then_inc(hidden2_made, 1)
            for n in range(M2):
                pe.wait_ge(hidden2_kept, n + 1)
                last = nc.tensor.matmul(y_ps, w3_sb[:, n:n + 1], hidden2_sb[:, n, :],
                                        start=n == 0, stop=n == M2 - 1)
            last.then_inc(y_made, 1)


def pair_of(order, i, j):
    return pair_index(min(order[i], order[j]), max(order[i], order[j])), order[i] < order[j]


def lay_out_w(w, order):
    flat = np.zeros((DIM, W_CHUNKS * CHUNK_TILES, QUAD, DIM), w.dtype)
    for k, (s, j, pairs) in enumerate(PASSES):
        for q, i in pairs.items():
            index, earlier = pair_of(order, i, j)
            flat[:, k, q, :] = w[:, index, :] if earlier else w[:, index, :].T
    flat = flat.reshape(DIM, W_CHUNKS, QUAD, STAGED * LANES)
    return np.ascontiguousarray(flat.transpose(1, 2, 0, 3).reshape(W_CHUNKS, LANES, STAGED * LANES))


def lay_out_w1(w1, order):
    rows = np.zeros((Z_CHUNKS, LANES, HIDDEN1), w1.dtype)
    for s, j, pairs in PASSES:
        chunk, group, row = z_place(s)
        for q, i in pairs.items():
            rows[chunk, DIM * group + row + q] = w1[pair_of(order, i, j)[0]]
    for half in range(2):
        start = DIM * (QUAD - 2 + half) + DENSE_ROW
        rows[-1, start:start + DENSE_HALF] = w1[ITEMS * (ITEMS - 1) // 2 + DENSE_HALF * half:][:DENSE_HALF]
    return rows


def kernel(**inputs):
    import concourse.bacc as bacc
    from concourse.bass_utils import run_bass_kernel_spmd

    given = {k: np.asarray(v) for k, v in inputs.items()}
    order = sorted(range(ITEMS), key=lambda f: given[f"tbl_{f}"].shape[0])
    short = order[:LOOKED_UP]
    assert all(given[f"tbl_{f}"].shape[0] == SHORT_ROWS for f in short)
    selecting = np.zeros((2 * DIM, (2 * QUAD - 1) * DIM), np.float32)
    for part in range(2):
        selecting[DIM * part:DIM * (part + 1), DIM * (QUAD - 1):DIM * QUAD] = np.eye(DIM)
    summing = np.zeros((LANES, WINDOW), np.float32)
    for q in range(QUAD):
        summing[DIM * q:DIM * (q + 1), DIM + q] = 1.0
    placing = np.zeros((DENSE, 2, DIM), np.float32)
    for k in range(DENSE):
        placing[k, k // DENSE_HALF, DENSE_ROW + k % DENSE_HALF] = 1.0
    arrays = {
        "dense_t": np.ascontiguousarray(given["dense_ctx"].T),
        "ids": given["ids"],
        "short_ids": np.ascontiguousarray(given["ids"][:, short].T),
        "short_tables": np.stack([given[f"tbl_{f}"] for f in short]),
        "table_rows": np.arange(SHORT_ROWS, dtype=np.float32).reshape(CHUNK_ROWS, TABLE_CHUNKS),
        "w_tiles": lay_out_w(given["L0_rec_w"], order),
        "w1": lay_out_w1(given["W_top1"], order),
        "b1": np.ascontiguousarray(given["b_top1"].reshape(M1, LANES).T),
        "w2": given["W_top2"],
        "b2": np.ascontiguousarray(given["b_top2"].reshape(M2, LANES).T),
        "w3": np.ascontiguousarray(given["W_top3"].reshape(M2, LANES).T),
        "identity": np.eye(LANES, dtype=np.float32),
        "summing": summing,
        "placing": placing,
        "selecting": selecting,
    }
    arrays.update({f"tbl_{f}": given[f"tbl_{f}"] for f in order[LOOKED_UP:]})

    nc = bacc.Bacc("TRN2", target_bir_lowering=False, num_devices=1)
    aps = {name: nc.dram_tensor(f"in_{name}", a.shape, mybir.dt.from_np(a.dtype), kind="ExternalInput").ap()
           for name, a in arrays.items()}
    out = nc.dram_tensor("out_y", (1, BATCH), mybir.dt.float32, kind="ExternalOutput").ap()
    tables = {j: aps.pop(f"tbl_{order[j]}") for j in range(LOOKED_UP, ITEMS)}
    build(nc, order=order, tables=tables, out=out, **aps)
    run = run_bass_kernel_spmd(nc, [{f"in_{name}": a for name, a in arrays.items()}], core_ids=[0])
    return run.results[0]["out_y"].reshape(BATCH, 1)
```
